# Optimizing a Trainium2 kernel written in Bass

```python
import numpy as np
import jax
import jax.numpy as jnp

def _softmax(x, axis=-1):
    return jax.nn.softmax(x, axis=axis)

def _gelu(x):
    return jax.nn.gelu(x, approximate=True)

def _silu(x):
    return jax.nn.silu(x)

def _sigmoid(x):
    return jax.nn.sigmoid(x)

def _layernorm(x, axis=-1, eps=1e-05):
    m = jnp.mean(x, axis=axis, keepdims=True)
    v = jnp.var(x, axis=axis, keepdims=True)
    return (x - m) / jnp.sqrt(v + eps)

def _scatter_add(tgt, idx, src, axis=0):
    return tgt.at[idx].add(src)

def _segment_sum(src, seg, n):
    return jax.ops.segment_sum(src, seg, n)
kernel_name = 'mk_xattn_ffn_d1_seqx_r4_84614f'

def setup_inputs(seed: int=0):
    np.random.seed(seed)
    _w = jnp.asarray

    def _rec_inputs():
        import jax
        import jax.numpy as jnp
        _rk = jax.random.key(seed)
        x = 7.22e-05 + 1 * jax.random.normal(jax.random.fold_in(_rk, 1), (8, 512, 512), jnp.float32)
        _lenS = 512 - jax.random.randint(jax.random.fold_in(_rk, 7), (8,), 0, max(1, 512 // 4) + 1, jnp.int32)
        _lenS2 = 64 - jax.random.randint(jax.random.fold_in(_rk, 8), (8,), 0, max(1, 64 // 4) + 1, jnp.int32)
        _ctx_512P = jax.random.normal(jax.random.fold_in(_rk, 11), (8, 16, 128), jnp.float32)
        _ctx_512c = jax.random.dirichlet(jax.random.fold_in(_rk, 511), 0.3 * jnp.ones((16,), jnp.float32), (8, 64))
        _ctx_512t = jnp.einsum('bsk,bkd->bsd', _ctx_512c, _ctx_512P)
        _ctx_512t = _ctx_512t * jax.lax.rsqrt(jnp.mean(jnp.square(_ctx_512t)) + 1e-12) * 0.953939
        ctx_512 = -0.000514642 + 1.00011 * (_ctx_512t + 0.3 * jax.random.normal(jax.random.fold_in(_rk, 611), (8, 64, 128), jnp.float32))
        return (x, ctx_512)
    x, ctx_512 = _rec_inputs()

    def _L0_xattn_setup():
        import jax, jax.numpy as jnp
        import numpy as np
        B, S, H, NH, L = (2, 512, 512, 16, 128)
        HD = H // NH
        key = jax.random.key(seed)
        k1, k2, k3, k4, k5 = jax.random.split(key, 5)
        scale = 0.02
        return {'q': jax.random.normal(k1, (B, S, H), dtype=jnp.float32), 'latent_kv': jax.random.normal(k2, (B, S, L), dtype=jnp.float32), 'Wq': jax.random.normal(k3, (H, H), dtype=jnp.float32) * scale, 'Wkv_expand': jax.random.normal(k4, (2 * H, L), dtype=jnp.float32) * scale, 'Wout': jax.random.normal(k5, (H, H), dtype=jnp.float32) * scale}
    _L0_xattn_all = _L0_xattn_setup()
    _L0_xattn_in = {k: v for k, v in _L0_xattn_all.items() if k in ('Wq', 'Wkv_expand', 'Wout')}
    del _L0_xattn_all

    def _L0_ffn_setup():
        import jax, jax.numpy as jnp
        import numpy as np
        H = 512
        E = 8
        K = 2
        I = 256
        NS = 1
        B, S = (2, 512)
        key = jax.random.key(seed)
        ks = jax.random.split(key, 12)
        std = 0.02
        return {'hidden_states': jax.random.normal(ks[0], (B, S, H), dtype=jnp.float32), 'router_w': jax.random.normal(ks[1], (E, H), dtype=jnp.float32) * std, 'wg': jax.random.normal(ks[2], (E, H, I), dtype=jnp.float32) * std, 'wu': jax.random.normal(ks[3], (E, H, I), dtype=jnp.float32) * std, 'wd': jax.random.normal(ks[4], (E, I, H), dtype=jnp.float32) * std, 'sg_w': jax.random.normal(ks[5], (H, I * NS), dtype=jnp.float32) * std, 'sg_b': jnp.zeros((I * NS,), dtype=jnp.float32), 'su_w': jax.random.normal(ks[6], (H, I * NS), dtype=jnp.float32) * std, 'su_b': jnp.zeros((I * NS,), dtype=jnp.float32), 'sd_w': jax.random.normal(ks[7], (I * NS, H), dtype=jnp.float32) * std, 'sd_b': jnp.zeros((H,), dtype=jnp.float32)}
    _L0_ffn_all = _L0_ffn_setup()
    _L0_ffn_in = {k: v for k, v in _L0_ffn_all.items() if k in ('router_w', 'wg', 'wu', 'wd', 'sg_w', 'sg_b', 'su_w', 'su_b', 'sd_w', 'sd_b')}
    del _L0_ffn_all
    return {'x': x, 'ctx_512': ctx_512, 'L0_xattn_Wq': _L0_xattn_in['Wq'], 'L0_xattn_Wkv_expand': _L0_xattn_in['Wkv_expand'], 'L0_xattn_Wout': _L0_xattn_in['Wout'], 'L0_ffn_router_w': _L0_ffn_in['router_w'], 'L0_ffn_wg': _L0_ffn_in['wg'], 'L0_ffn_wu': _L0_ffn_in['wu'], 'L0_ffn_wd': _L0_ffn_in['wd'], 'L0_ffn_sg_w': _L0_ffn_in['sg_w'], 'L0_ffn_sg_b': _L0_ffn_in['sg_b'], 'L0_ffn_su_w': _L0_ffn_in['su_w'], 'L0_ffn_su_b': _L0_ffn_in['su_b'], 'L0_ffn_sd_w': _L0_ffn_in['sd_w'], 'L0_ffn_sd_b': _L0_ffn_in['sd_b']}

def reference(x, ctx_512, L0_xattn_Wq, L0_xattn_Wkv_expand, L0_xattn_Wout, L0_ffn_router_w, L0_ffn_wg, L0_ffn_wu, L0_ffn_wd, L0_ffn_sg_w, L0_ffn_sg_b, L0_ffn_su_w, L0_ffn_su_b, L0_ffn_sd_w, L0_ffn_sd_b):
    import jax
    import jax.numpy as jnp

    def _L0_xattn_ref(q, latent_kv, Wq, Wkv_expand, Wout):
        import jax, jax.numpy as jnp
        import numpy as np
        B, S, H, NH, L = (2, 512, 512, 16, 128)
        HD = H // NH
        b, sq, _ = q.shape
        sk = latent_kv.shape[1]
        qp = q @ Wq.T
        kv = latent_kv @ Wkv_expand.T
        k, v = jnp.split(kv, 2, axis=-1)
        qh = qp.reshape(b, sq, NH, HD).transpose(0, 2, 1, 3)
        kh = k.reshape(b, sk, NH, HD).transpose(0, 2, 1, 3)
        vh = v.reshape(b, sk, NH, HD).transpose(0, 2, 1, 3)
        inv_sqrt_d = 1.0 / jnp.sqrt(jnp.float32(HD))
        scores = jnp.einsum('bhqd,bhkd->bhqk', qh, kh) * inv_sqrt_d
        causal = jnp.tril(jnp.ones((sq, sk), dtype=bool))
        scores = jnp.where(causal, scores, jnp.finfo(scores.dtype).min)
        attn = jax.nn.softmax(scores, axis=-1)
        out = jnp.einsum('bhqk,bhkd->bhqd', attn, vh)
        out = out.transpose(0, 2, 1, 3).reshape(b, sq, H)
        return out @ Wout.T

    def _L0_ffn_ref(hidden_states, router_w, wg, wu, wd, sg_w, sg_b, su_w, su_b, sd_w, sd_b):
        import jax, jax.numpy as jnp
        import numpy as np
        H = 512
        E = 8
        K = 2
        I = 256
        NS = 1
        B, S = (2, 512)
        x = hidden_states.reshape(-1, H)
        T = x.shape[0]
        logits = x @ router_w.T
        scores, top_idx = jax.lax.top_k(logits, K)
        comb = jnp.zeros((T, E), dtype=x.dtype).at[jnp.arange(T)[:, None], top_idx].set(scores)
        g = jnp.einsum('td,edi->eti', x, wg)
        u = jnp.einsum('td,edi->eti', x, wu)
        h = jax.nn.silu(g) * u
        y = jnp.einsum('eti,eid->etd', h, wd)
        moe_out = jnp.einsum('etd,te->td', y, comb)
        se = jax.nn.silu(x @ sg_w + sg_b) * (x @ su_w + su_b) @ sd_w + sd_b
        out = (moe_out + se).reshape(hidden_states.shape)
        return out
    x = x + _L0_xattn_ref(_layernorm(x, axis=-1), ctx_512, L0_xattn_Wq, L0_xattn_Wkv_expand, L0_xattn_Wout)
    x = x + _L0_ffn_ref(_layernorm(x, axis=-1), L0_ffn_router_w, L0_ffn_wg, L0_ffn_wu, L0_ffn_wd, L0_ffn_sg_w, L0_ffn_sg_b, L0_ffn_su_w, L0_ffn_su_b, L0_ffn_sd_w, L0_ffn_sd_b)
    return x

_drawn_inputs = setup_inputs


def setup_inputs(seed=0):
    import zlib

    import numpy as np

    out = dict(_drawn_inputs(seed))
    spreads = {'L0_ffn_sg_b': (0.0, 0.8), 'L0_ffn_su_b': (0.0, 0.8), 'L0_ffn_sd_b': (0.0, 0.1)}
    factors = {'L0_xattn_Wq': 23.894}
    for name, (base, spread) in spreads.items():
        noise = np.random.default_rng([zlib.crc32(name.encode()), seed]).standard_normal(out[name].shape)
        drawn = base * np.exp(spread * noise) if base else spread * noise
        out[name] = jnp.asarray(drawn.astype(out[name].dtype))
    for name, factor in factors.items():
        out[name] = (out[name] * factor).astype(out[name].dtype)
    return out
```

```python
import concourse.bass as bass
from concourse import mybir
from contextlib import ExitStack

F32 = mybir.dt.float32
I32 = mybir.dt.int32
U32 = mybir.dt.uint32
ALU = mybir.AluOpType
ACT = mybir.ActivationFunctionType
AX = mybir.AxisListType

P = 128
B, S, H = 8, 512, 512
NH, HD = 16, 32
SK, L = 64, 128
E, I = 8, 256
C = H // P
CI = I // P
PAIRS = NH // 2
HPC = P // HD
TPB = S // P
T = B * S // P
TOKENS = T * P
SLOTS = 2 * T + E
VW = HD + 1
EPS = 1e-5
BIG = 3.4e38
FAR = 8192.0
SCALE = float(HD) ** -0.5
AHEAD = 3
GU = C * 2 * I
WE = GU + CI * H
EARLY = 5


def xattn_moe(nc, x, ctxT, wqT, wkT, wvT, woT, routerT, experts, shared, sh_b, sd_b, out):
    xn_dram = nc.dram_tensor("normed_tokens", [TOKENS, H], F32, kind="Internal").ap()
    stack = ExitStack()
    with stack:
        def sb(name, shape, dt=F32):
            return stack.enter_context(nc.sbuf_tensor(name, shape, dt))

        def sem(name):
            return stack.enter_context(nc.semaphore(name))

        w_exp = sb("w_exp", [P, E, WE])
        w_sh = sb("w_sh", [P, WE])
        w_q = sb("w_q", [P, C, H])
        w_o = sb("w_o", [P, C, H])
        w_r = sb("w_r", [P, C, E])
        k_size = B * C * HPC * SK
        k_flat = w_exp[:, :, :].rearrange("p e w -> p (e w)")[:, E * WE - k_size:]
        k_bd = k_flat.rearrange("p (b c h k) -> p b c h k", b=B, c=C, h=HPC)
        v_bd = sb("v_bd", [P, B, PAIRS, 2, VW])
        ident = sb("ident", [P, P])
        sh_bias = sb("sh_bias", [P, 2 * I])
        sd_bias = sb("sd_bias", [P, H])
        mask = sb("mask", [P, SK])
        minus_half = sb("minus_half", [P, 1])
        ones_row = sb("ones_row", [1, P])
        x_in = sb("x_in", [P, 4, H])
        xn1 = sb("xn1", [P, H])
        xn1T = sb("xn1T", [P, C, P])
        qT = sb("qT", [P, C, P])
        probs = sb("probs", [P, NH, SK])
        probsT = sb("probsT", [P, PAIRS, P])
        attn = sb("attn", [P, NH, HD])
        attnT = sb("attnT", [P, C, P])
        x1 = sb("x1", [P, H])
        x1b = sb("x1b", [P, 2, H])
        xn2 = sb("xn2", [P, 2, H])
        xn2T = sb("xn2T", [P, C, P])
        gate_up = sb("gate_up", [P, 2 * I])
        tanh_g = sb("tanh_g", [P, I])
        hid = sb("hid", [P, I])
        hidT = sb("hidT", [P, CI, P])
        base = sb("base", [P, 2, H])
        stats = sb("stats", [P, 2, 6])
        moments = sb("moments", [P, 2, 2])
        rstd = sb("rstd", [P, 2, 2])
        recip = sb("recip", [P, NH])
        head_max = sb("head_max", [P, NH])
        logits = sb("logits", [P, T, E])
        gather_at = sb("gather_at", [P, SLOTS], U32)
        add_at = sb("add_at", [P, SLOTS], U32)
        weight_at = sb("weight_at", [P, SLOTS])
        expert_of = sb("expert_of", [1, SLOTS], I32)
        gather_now = sb("gather_now", [P, 4], U32)
        add_now = sb("add_now", [P, 2], U32)
        v_flat = v_bd[:, :, :, :, :].rearrange("p b r h w -> p (b r h w)")
        TE = T * E

        def scratch(n):
            return v_flat[:, n * TE:(n + 1) * TE]

        (eq, oneh1, oneh2, second, both, totals, ones_te, cum, before, rank_all, selected,
         steps128, rev) = [scratch(n) for n in range(13)]
        te = dict(t=T, e=E)
        small = sb("small", [P, 8 * T])
        picked = sb("picked", [P, 6, 2, T])
        picked_i = sb("picked_i", [P, 2, 2, T], I32)
        tri = xn1[:, 0:P]
        ones_pp = xn1[:, P:2 * P]
        iota_p = xn1[:, 2 * P:3 * P]
        iota_s = xn1[:, 3 * P:3 * P + SLOTS]
        token_no = small[:, 0:T]
        hot_lo = probs[:, :, :].rearrange("p h k -> p (h k)")[:, 0:4 * P].rearrange("p (n q) -> p n q", n=4)
        hot_hi = probsT[:, :, :].rearrange("p r q -> p (r q)")[:, 0:8 * SLOTS].rearrange(
            "p (n v s) -> p n v s", n=4, v=2)
        le_tab = x_in[0:1, :, :].rearrange("p a h -> p (a h)")[:, 0:SLOTS * E].rearrange("p (s e) -> p s e", e=E)
        y = base
        silu_g = tanh_g
        ctx_sb = x_in[:, 0:2, :].rearrange("p a h -> p (a h)").rearrange("p (b d k) -> p b d k", b=B, d=2)
        wk_sb = x_in[:, 2, :]
        wv_sb = x_in[:, 3, :]
        bias_rows = base[0:1, :, :]

        psum = stack.enter_context(nc.psum_tensor("psum", [P, 8, 512], F32))

        def bank(n, k=1):
            return psum[:, n:n + k, :].rearrange("p n w -> p (n w)")

        ctx_in = sem("ctx_in")
        waits_met = sem("waits_met")
        wq_in, wo_in, wsh_in, experts_in, experts_late_in = [sem(n) for n in (
            "wq_in", "wo_in", "wsh_in", "experts_in", "experts_late_in")]
        const_made, const_ready, kv_zeroed = sem("const_made"), sem("const_ready"), sem("kv_zeroed")
        k_mm, bias_mm, v_mm, bias_copied, kv_copied, v_copied = [sem(n) for n in (
            "k_mm", "bias_mm", "v_mm", "bias_copied", "kv_copied", "v_copied")]
        x_loaded = [sem(f"x_loaded{i}") for i in range(4)]
        ln1_chain, ln1_var, ln1_rstd, ln2_chain, ln2_var, ln2_rstd, ln1_eps, ln2_eps = [sem(n) for n in (
            "ln1_chain", "ln1_var", "ln1_rstd", "ln2_chain", "ln2_var", "ln2_rstd", "ln1_eps", "ln2_eps")]
        xn1_ready, xn1T_mm, xn1T_ready, q_mm, qT_ready = [sem(n) for n in (
            "xn1_ready", "xn1T_mm", "xn1T_ready", "q_mm", "qT_ready")]
        scores_mm, masked, max_ready, shifted, probs_ready = [sem(n) for n in (
            "scores_mm", "masked", "max_ready", "shifted", "probs_ready")]
        probsT_mm, probsT_ready, av_mm, recip_ready, attn_ready = [sem(n) for n in (
            "probsT_mm", "probsT_ready", "av_mm", "recip_ready", "attn_ready")]
        attnT_mm, attnT_ready, proj_mm, x1_ready, x1b_ready = [sem(n) for n in (
            "attnT_mm", "attnT_ready", "proj_mm", "x1_ready", "x1b_ready")]
        xn2_ready, xn2T_mm, xn2T_ready, gu_mm, gu_ready, tanh_ready = [sem(n) for n in (
            "xn2_ready", "xn2T_mm", "xn2T_ready", "gu_mm", "gu_ready", "tanh_ready")]
        hid_chain, hid_ready, hidT_mm, hidT_ready, down_mm, base_ready = [sem(n) for n in (
            "hid_chain", "hid_ready", "hidT_mm", "hidT_ready", "down_mm", "base_ready")]
        xn2_stored = [sem(f"xn2_stored{i}") for i in range(2)]
        base_stored = [sem(f"base_stored{i}") for i in range(2)]
        route_const, route_chain, both_ready, rank_mm = [sem(n) for n in (
            "route_const", "route_chain", "both_ready", "rank_mm")]
        hot_ready, hot_used, list_ready = [sem(n) for n in (
            "hot_ready", "hot_used", "list_ready")]
        gather_set, add_set = sem("gather_set"), sem("add_set")
        gathered = [sem(f"gathered{i}") for i in range(4)]
        xg_mm, xgT_ready, egu_mm, silu_ready, ehid_ready, ehidT_mm, ehidT_ready, edown_mm, y_ready, y_added = [
            sem(n) for n in ("xg_mm", "xgT_ready", "egu_mm", "silu_ready", "ehid_ready", "ehidT_mm",
                             "ehidT_ready", "edown_mm", "y_ready", "y_added")]

        def live(tile):
            return not isinstance(tile, int) or 0 <= tile < T

        def wait(eng, semaphore, value):
            if not isinstance(value, int) or value > 0:
                eng.wait_ge(semaphore, value)

        def plain(eng):
            eng.sem_inc(waits_met, 1)

        def over_tiles(eng, step, behind):
            for b in range(2):
                for j in range(TPB):
                    step(b, j)
            with eng.Fori(2, B) as b:
                for j in range(TPB):
                    step(b, j)
            for j in range(behind):
                step(B, j)

        def elive(tile):
            return not isinstance(tile, int) or 0 <= tile < SLOTS

        def over_list(eng, step, behind):
            for j in range(4):
                step(0, j)
            with eng.Fori(1, SLOTS // 4) as q:
                for j in range(4):
                    step(q, j)
            for j in range(behind):
                step(SLOTS // 4, j)

        block = stack.enter_context(nc.Block())

        @block.sync
        def _(sp):
            sp.dma_start(ctx_sb[:, :, 0, :], ctxT).then_inc(ctx_in, 16)
            sp.dma_start(ctx_sb[:, :, 1, :], ctxT).then_inc(ctx_in, 16)
            sp.dma_start(wk_sb, wkT).then_inc(ctx_in, 16)
            sp.dma_start(wv_sb, wvT).then_inc(ctx_in, 16)
            sp.dma_start(bias_rows[:, 0, :], sh_b).then_inc(ctx_in, 16)
            sp.dma_start(bias_rows[:, 1, :], sd_b).then_inc(ctx_in, 16)
            sp.dma_start(w_q[:, :, :], wqT).then_inc(wq_in, 16)
            sp.dma_start(w_r[:, :, :], routerT).then_inc(wq_in, 16)
            sp.wait_ge(v_mm, B)

            def step(b, j):
                tile = TPB * b + j
                wait(sp, x1_ready, tile - 3)
                sp.dma_start(x_in[:, j, :], x[bass.ds(tile * P, P), :]).then_inc(x_loaded[j], 16)

            def weights(b, j):
                if b == 0 and j == 1:
                    sp.dma_start(w_o[:, :, :], woT).then_inc(wo_in, 16)
                    sp.dma_start(w_sh[:, :], shared).then_inc(wsh_in, 16)
                if b == 1 and j == 0:
                    for e in range(EARLY):
                        sp.dma_start(w_exp[:, e, :], experts[:, e, :]).then_inc(experts_in, 16)

            for b in range(2):
                for j in range(TPB):
                    step(b, j)
                    weights(b, j)
            with sp.Fori(2, B) as b:
                for j in range(TPB):
                    step(b, j)
            sp.wait_ge(scores_mm, T)
            for e in range(EARLY, E):
                sp.dma_start(w_exp[:, e, :], experts[:, e, :]).then_inc(experts_late_in, 16)

        @block.gpsimd
        def _(pool):
            pool.memset(ident[:, :], 0.0).then_inc(const_made, 1)
            pool.memset(mask[:, :], BIG).then_inc(const_made, 1)
            pool.memset(minus_half[:, :], -0.5).then_inc(const_made, 1)
            pool.memset(ones_row[:, :], 1.0).then_inc(const_ready, 1)
            pool.wait_ge(const_made, 3)
            pool.affine_select(out=ident[:, :], in_=ident[:, :], compare_op=ALU.not_equal, fill=1.0, base=0,
                               pattern=[[-1, P]], channel_multiplier=1).then_inc(const_ready, 1)
            pool.affine_select(out=mask[:, :], in_=mask[:, :], compare_op=ALU.is_ge, fill=-BIG, base=0,
                               pattern=[[-1, SK]], channel_multiplier=1).then_inc(const_ready, 1)
            pool.memset(k_flat, 0.0).then_inc(kv_zeroed, 1)

            def inv_std(which, tile, var, eps_added, out_sem):
                pool.wait_ge(var, tile + 1)
                plain(pool)
                pool.tensor_scalar(rstd[:, which, 0:1], moments[:, which, 1:2], EPS, None, ALU.add).then_inc(eps_added, 1)
                pool.wait_ge(eps_added, tile + 1)
                pool.tensor_tensor(rstd[:, which, 1:2], rstd[:, which, 0:1], minus_half[:, :],
                                   ALU.pow).then_inc(out_sem, 1)

            pool.wait_ge(bias_copied, 2)

            def step(b, j):
                tile = TPB * b + j
                t3 = tile - 3
                if live(t3):
                    inv_std(1, t3, ln2_var, ln2_eps, ln2_rstd)
                if live(tile):
                    inv_std(0, tile, ln1_var, ln1_eps, ln1_rstd)
                if live(t3):
                    pool.wait_ge(x1_ready, t3 + 1)
                    wait(pool, base_ready, t3 - 1)
                    pool.tensor_tensor(x1b[:, (j - 3) % 2, :], x1[:, :], sd_bias[:, :], ALU.add).then_inc(x1b_ready, 1)

            over_tiles(pool, step, 3)

            pool.wait_ge(av_mm, T)
            pool.wait_ge(xn1T_mm, T)
            pool.memset(tri, 1.0).then_inc(route_const, 1)
            pool.memset(ones_pp, 1.0).then_inc(route_const, 1)
            pool.wait_ge(route_const, 1)
            pool.affine_select(out=tri, in_=tri, compare_op=ALU.is_ge, fill=0.0, base=-1,
                               pattern=[[1, P]], channel_multiplier=-1).then_inc(route_const, 1)
            pool.iota(iota_p, pattern=[[1, P]], base=0, channel_multiplier=0,
                      allow_small_or_imprecise_dtypes=True).then_inc(route_const, 1)
            pool.iota(iota_s, pattern=[[1, SLOTS]], base=0, channel_multiplier=0,
                      allow_small_or_imprecise_dtypes=True).then_inc(route_const, 1)
            pool.iota(token_no, pattern=[[P, T]], base=1, channel_multiplier=1,
                      allow_small_or_imprecise_dtypes=True).then_inc(route_const, 1)
            pool.iota(rev.rearrange("p (t e) -> p t e", **te), pattern=[[0, T], [-1, E]], base=E, channel_multiplier=0,
                      allow_small_or_imprecise_dtypes=True).then_inc(route_const, 1)
            pool.iota(steps128.rearrange("p (e t) -> p e t", **te), pattern=[[0, E], [P, T]], base=0,
                      channel_multiplier=0, allow_small_or_imprecise_dtypes=True).then_inc(route_const, 1)

            pool.wait_ge(list_ready, 1)
            for i in range(2):
                pool.wait_ge(xn2_stored[i], 16 * T // 2)
                pool.wait_ge(base_stored[i], 16 * T // 2)

            def gather(tile, ring):
                wait(pool, xg_mm, tile - 3)
                pool.tensor_copy(gather_now[:, ring:ring + 1], gather_at[:, bass.ds(tile, 1)]).then_inc(gather_set, 1)
                pool.wait_ge(gather_set, tile + 1)
                plain(pool)
                pool.indirect_dma_start(x_in[:, ring, :], None, xn_dram,
                                        bass.IndirectOffsetOnAxis(gather_now[:, ring:ring + 1], 0)).then_inc(gathered[ring], 16)

            def add(tile, ring):
                pool.tensor_copy(add_now[:, ring:ring + 1], add_at[:, bass.ds(tile, 1)]).then_inc(add_set, 1)
                pool.wait_ge(add_set, tile + 1)
                pool.wait_ge(y_ready, tile + 1)
                wait(pool, y_added, 16 * tile)
                plain(pool)
                pool.indirect_dma_start(out, bass.IndirectOffsetOnAxis(add_now[:, ring:ring + 1], 0),
                                        y[:, ring, :], None, bounds_check=TOKENS - 1, oob_is_err=False,
                                        compute_op=ALU.add).then_inc(y_added, 16)

            for t in range(8):
                gather(t, t % 4)
                if t >= 6:
                    add(t - 6, t % 2)
            with pool.Fori(2, SLOTS // 4) as q:
                for j in range(4):
                    gather(4 * q + j, j)
                    add(4 * q + (j - 6), j % 2)
            for t in range(SLOTS, SLOTS + 6):
                add(t - 6, t % 2)
            pool.wait_ge(y_added, 16 * SLOTS)

        @block.scalar
        def _(act):
            act.wait_ge(bias_mm, 2)
            act.activation(sh_bias[:, :], bank(4), ACT.Copy).then_inc(bias_copied, 1)
            act.activation(sd_bias[:, :], bank(5), ACT.Copy).then_inc(bias_copied, 1)

            def step(b, j):
                tile = TPB * b + j
                t2, t3, t4 = tile - 2, tile - 3, tile - 4
                if live(t2):
                    act.wait_ge(probsT_mm, t2 + 1)
                    act.activation(probsT[:, :, :], bank(2, 2), ACT.Copy).then_inc(probsT_ready, 1)
                if live(t3):
                    act.wait_ge(xn2T_mm, t3 + 1)
                    act.activation(xn2T[:, :, :], bank(4), ACT.Copy).then_inc(xn2T_ready, 1)
                    act.wait_ge(xn2_ready, t3 + 1)
                    act.dma_start(xn_dram[bass.ds(t3 * P, P), :], xn2[:, (j - 3) % 2, :]
                                  ).then_inc(xn2_stored[(j - 3) % 2], 16)
                if live(tile):
                    act.wait_ge(xn1T_mm, tile + 1)
                    act.activation(xn1T[:, :, :], bank(5), ACT.Copy).then_inc(xn1T_ready, 1)
                if live(tile - 1):
                    act.wait_ge(shifted, tile)
                    act.activation(probs[:, :, :], probs[:, :, :], ACT.Exp, scale=SCALE).then_inc(probs_ready, 1)
                if live(t4):
                    act.wait_ge(base_ready, t4 + 1)
                    act.dma_start(out[bass.ds(t4 * P, P), :], base[:, j % 2, :]).then_inc(base_stored[j % 2], 16)
                if live(t3):
                    act.wait_ge(gu_ready, t3 + 1)
                    act.activation(tanh_g[:, :], gate_up[:, 0:I], ACT.Tanh, scale=0.5).then_inc(tanh_ready, 1)
                if live(t2):
                    act.wait_ge(attnT_mm, t2 + 1)
                    act.activation(attnT[:, :, :], bank(6), ACT.Copy).then_inc(attnT_ready, 1)
                if live(tile):
                    act.wait_ge(q_mm, tile + 1)
                    act.activation(qT[:, :, :], bank(7), ACT.Copy).then_inc(qT_ready, 1)
                if live(t3):
                    act.wait_ge(hidT_mm, t3 + 1)
                    act.activation(hidT[:, :, :], psum[:, 3, 0:I], ACT.Copy).then_inc(hidT_ready, 1)
                    act.activation(logits[:, bass.ds(t3, 1), :], psum[:, 3, I:I + E], ACT.Copy).then_inc(hidT_ready, 1)

            over_tiles(act, step, 4)

            def estep(q, j):
                t = 4 * q + j
                if elive(t - 1):
                    act.wait_ge(egu_mm, t)
                    act.activation(silu_g[:, :], psum[:, 1, 0:I], ACT.Silu).then_inc(silu_ready, 1)
                if elive(t):
                    act.wait_ge(xg_mm, t + 1)
                    act.activation(xn2T[:, :, :], bank(0), ACT.Copy).then_inc(xgT_ready, 1)
                if elive(t - 1):
                    act.wait_ge(ehidT_mm, t)
                    act.activation(hidT[:, :, :], psum[:, 2, 0:I], ACT.Copy).then_inc(ehidT_ready, 1)

            over_list(act, estep, 1)

        @block.vector
        def _(dve):
            dve.memset(v_bd[:, :, :, :, :], 0.0).then_inc(kv_zeroed, 1)
            dve.wait_ge(kv_zeroed, 2)
            dve.memset(v_bd[0:SK, :, :, 0, HD:VW], 1.0).then_inc(kv_copied, 1)
            dve.memset(v_bd[SK:P, :, :, 1, HD:VW], 1.0).then_inc(kv_copied, 1)
            dve.wait_ge(k_mm, 1)
            for c in range(C):
                for h in range(HPC):
                    rows = slice(HD * h, HD * h + HD)
                    dve.tensor_copy(k_bd[rows, :, c, h, :],
                                    psum[rows, c, :].rearrange("p (b k) -> p b k", b=B)).then_inc(kv_copied, 1)
            for b in range(B):
                dve.wait_ge(v_mm, b + 1)
                for h in range(2):
                    rows = slice(SK * h, SK * h + SK)
                    dve.tensor_copy(v_bd[rows, b, :, h, 0:HD], psum[rows, 6 + b % 2, :].rearrange(
                        "p (r h d) -> p r h d", h=2, d=HD)[:, :, h, :]).then_inc(v_copied, 1)

            def stage_stats(which, src, chain, var, tile):
                dve.bn_stats(stats[:, which, :], src).then_inc(chain, 1)
                dve.wait_ge(chain, tile + 1)
                plain(dve)
                dve.bn_aggr(moments[:, which, :], stats[:, which, :]).then_inc(var, 1)

            def step(b, j):
                tile = TPB * b + j
                t1, t2, t3, t4 = tile - 1, tile - 2, tile - 3, tile - 4
                if live(t3):
                    dve.wait_ge(proj_mm, t3 + 1)
                    wait(dve, x1b_ready, t3)
                    dve.tensor_tensor(x1[:, :], bank(2), x_in[:, (j - 3) % 4, :], ALU.add).then_inc(x1_ready, 1)
                    dve.wait_ge(x1_ready, t3 + 1)
                    stage_stats(1, x1[:, :], ln2_chain, ln2_var, t3)
                if live(tile):
                    dve.wait_ge(x_loaded[j], 16 * (b + 1))
                    stage_stats(0, x_in[:, j, :], ln1_chain, ln1_var, tile)
                if live(t3):
                    uses = (TPB // 2) * b + (j - 3) // 2
                    wait(dve, xn2_stored[(j - 3) % 2], 16 * uses)
                    dve.wait_ge(ln2_rstd, t3 + 1)
                    dve.tensor_scalar(xn2[:, (j - 3) % 2, :], x1[:, :], moments[:, 1, 0:1], rstd[:, 1, 1:2],
                                      ALU.subtract, ALU.mult).then_inc(xn2_ready, 1)
                if live(tile):
                    dve.wait_ge(ln1_rstd, tile + 1)
                    wait(dve, xn1T_mm, tile)
                    dve.tensor_scalar(xn1[:, :], x_in[:, j, :], moments[:, 0, 0:1], rstd[:, 0, 1:2],
                                      ALU.subtract, ALU.mult).then_inc(xn1_ready, 1)
                if live(t4):
                    dve.wait_ge(down_mm, t4 + 1)
                    dve.wait_ge(x1b_ready, t4 + 1)
                    uses = (TPB // 2) * (b - 1) + j // 2
                    wait(dve, base_stored[j % 2], 16 * uses)
                    dve.tensor_tensor(base[:, j % 2, :], bank(5), x1b[:, j % 2, :], ALU.add).then_inc(base_ready, 1)
                if live(t1):
                    dve.wait_ge(scores_mm, t1 + 1)
                    wait(dve, probsT_mm, t1)
                    scores = bank(0, 2).rearrange("p (h k) -> p h k", k=SK)
                    if (j - 1) % TPB == 0:
                        dve.tensor_tensor(probs[:, :, :], scores, mask[:, None, :].to_broadcast([P, NH, SK]),
                                          ALU.min).then_inc(masked, 1)
                        dve.wait_ge(masked, b + 1)
                        scores = probs[:, :, :]
                    dve.tensor_reduce(head_max[:, :], scores, AX.X, ALU.max).then_inc(max_ready, 1)
                    dve.wait_ge(max_ready, t1 + 1)
                    dve.tensor_tensor(probs[:, :, :], scores, head_max[:, :, None].to_broadcast([P, NH, SK]),
                                      ALU.subtract).then_inc(shifted, 1)
                if live(t2):
                    dve.wait_ge(av_mm, t2 + 1)
                    av = psum[:, 6:8, 0:4 * 2 * VW].rearrange("p n (q w) -> p n q w", w=VW)
                    dve.reciprocal(recip[:, :].rearrange("p (n q) -> p n q", n=2), av[:, :, :, HD]).then_inc(recip_ready, 1)
                    dve.wait_ge(recip_ready, t2 + 1)
                    wait(dve, attnT_mm, t2)
                    dve.tensor_tensor(attn[:, :, :].rearrange("p (n q) d -> p n q d", n=2), av[:, :, :, 0:HD],
                                      recip[:, :].rearrange("p (n q) -> p n q", n=2)[:, :, :, None].to_broadcast(
                                          [P, 2, NH // 2, HD]), ALU.mult).then_inc(attn_ready, 1)
                if live(t3):
                    dve.wait_ge(gu_mm, t3 + 1)
                    dve.tensor_tensor(gate_up[:, :], bank(4), sh_bias[:, :], ALU.add).then_inc(gu_ready, 1)
                    dve.wait_ge(tanh_ready, t3 + 1)
                    dve.scalar_tensor_tensor(tanh_g[:, :], tanh_g[:, :], 1.0, gate_up[:, 0:I],
                                             ALU.add, ALU.mult).then_inc(hid_chain, 1)
                    dve.wait_ge(hid_chain, t3 + 1)
                    wait(dve, hidT_mm, t3)
                    dve.scalar_tensor_tensor(hid[:, :], tanh_g[:, :], 0.5, gate_up[:, I:2 * I],
                                             ALU.mult, ALU.mult).then_inc(hid_ready, 1)

            dve.wait_ge(bias_copied, 2)
            dve.wait_ge(const_ready, 3)
            over_tiles(dve, step, 4)

            links = [0]

            def link(ins):
                links[0] += 1
                ins.then_inc(route_chain, 1)
                dve.wait_ge(route_chain, links[0])

            def by_te(a):
                return a.rearrange("p (t e) -> p t e", **te)

            def by_et(a):
                return a.rearrange("p (e t) -> p e t", **te)

            def over_e(a):
                return a[:, :, None].to_broadcast([P, T, E])

            dve.wait_ge(hidT_ready, 2 * T)
            dve.wait_ge(route_const, 8)
            lg = logits[:, :, :]
            best = picked[:, 0, :, :]
            top = small[:, 2 * T:3 * T]

            def pick(values, k, oneh):
                link(dve.tensor_reduce(best[:, k, :], values, AX.X, ALU.max))
                link(dve.tensor_tensor(by_te(eq), values, over_e(best[:, k, :]), ALU.is_equal))
                link(dve.tensor_tensor(eq, eq, rev, ALU.mult))
                link(dve.tensor_reduce(top, by_te(eq), AX.X, ALU.max))
                link(dve.tensor_tensor(by_te(oneh), by_te(eq), over_e(top), ALU.is_equal))

            pick(lg, 0, oneh1)
            link(dve.scalar_tensor_tensor(second, oneh1, -BIG, logits[:, :, :].rearrange("p t e -> p (t e)"),
                                          ALU.mult, ALU.add))
            pick(by_te(second), 1, oneh2)
            dve.tensor_tensor(both, oneh1, oneh2, ALU.add).then_inc(both_ready, 1)
            link(dve.memset(ones_te, 1.0))
            link(dve.memset(by_et(ones_te)[:, :, 0:1], 0.0))
            dve.wait_ge(rank_mm, 1)
            rank = psum[:, 0, 0:TE]
            link(dve.tensor_copy(by_et(totals), by_te(psum[:, 0, TE:2 * TE]).rearrange("p t e -> p e t")))
            link(dve.tensor_tensor_scan(cum, ones_te, totals, 0.0, ALU.mult, ALU.add))
            link(dve.tensor_tensor(before, cum, totals, ALU.subtract))
            link(dve.tensor_tensor(by_te(rank_all), by_te(rank), by_et(before).rearrange("p e t -> p t e"), ALU.add))
            n_tiles, t_cum, t_before, ones_e = [small[:, 3 * T + 8 * n:3 * T + 8 * n + E] for n in range(4)]
            link(dve.tensor_tensor(by_et(eq), by_et(cum)[:, :, T - 1:T].to_broadcast([P, E, T]), by_et(steps128), ALU.is_gt))
            link(dve.tensor_reduce(n_tiles, by_et(eq), AX.X, ALU.add))
            link(dve.memset(ones_e, 1.0))
            link(dve.tensor_tensor_scan(t_cum, ones_e, n_tiles, 0.0, ALU.mult, ALU.add))
            link(dve.tensor_tensor(t_before, t_cum, n_tiles, ALU.subtract))
            link(dve.tensor_tensor(le_tab, t_cum[0:1, None, :].to_broadcast([1, SLOTS, E]),
                                   iota_s[0:1, :, None].to_broadcast([1, SLOTS, E]), ALU.is_le))
            exp_f = small[0:1, 4 * T:4 * T + SLOTS]
            link(dve.tensor_reduce(exp_f, le_tab, AX.X, ALU.add))
            link(dve.tensor_scalar(expert_of[:, :], exp_f, float(E - 1), None, ALU.min))
            within, first, lo, hi = [picked[:, n, :, :] for n in (1, 2, 3, 4)]
            for k, oneh in enumerate((oneh1, oneh2)):
                link(dve.tensor_tensor(selected, oneh, rank_all, ALU.mult))
                link(dve.tensor_reduce(within[:, k, :], by_te(selected), AX.X, ALU.add))
                link(dve.tensor_tensor(by_te(selected), by_te(oneh), t_before[:, None, :].to_broadcast([P, T, E]), ALU.mult))
                link(dve.tensor_reduce(first[:, k, :], by_te(selected), AX.X, ALU.add))
            link(dve.tensor_copy(picked_i[:, 0, :, :], within))
            link(dve.tensor_scalar(picked_i[:, 1, :, :], picked_i[:, 0, :, :], P - 1, None, ALU.bitwise_and))
            link(dve.tensor_copy(lo, picked_i[:, 1, :, :]))
            link(dve.tensor_scalar(picked_i[:, 1, :, :], picked_i[:, 0, :, :], 7, None, ALU.arith_shift_right))
            link(dve.tensor_copy(hi, picked_i[:, 1, :, :]))
            link(dve.tensor_tensor(hi, hi, first, ALU.add))

            def hot(t, k, n):
                col = bass.ds(t, 1)
                dve.tensor_scalar(hot_lo[:, n, :], iota_p, lo[:, k, col], None, ALU.is_equal)
                dve.tensor_scalar(hot_hi[:, n, 0, :], iota_s, hi[:, k, col], token_no[:, col], ALU.is_equal, ALU.mult)
                dve.tensor_scalar(hot_hi[:, n, 1, :], iota_s, hi[:, k, col], best[:, k, col],
                                  ALU.is_equal, ALU.mult).then_inc(hot_ready, 1)

            for t in range(2):
                for k in range(2):
                    hot(t, k, 2 * t + k)
            with dve.Fori(1, T // 2) as pair:
                for i in range(2):
                    for k in range(2):
                        dve.wait_ge(hot_used, 4 * pair + (2 * i + k - 3))
                        hot(2 * pair + i, k, 2 * i + k)
            dve.wait_ge(hot_used, 2 * T)
            token1 = psum[:, 1, 0:SLOTS]
            fl = [hid[:, n * SLOTS:(n + 1) * SLOTS] for n in range(3)]
            link(dve.tensor_copy(weight_at[:, :], psum[:, 1, SLOTS:2 * SLOTS]))
            link(dve.tensor_scalar(fl[0], token1, 1.0, 0.0, ALU.subtract, ALU.max))
            link(dve.tensor_copy(gather_at[:, :], fl[0]))
            link(dve.tensor_scalar(fl[1], token1, 0.0, FAR, ALU.is_equal, ALU.mult))
            link(dve.tensor_tensor(fl[2], fl[1], fl[0], ALU.add))
            dve.tensor_copy(add_at[:, :], fl[2]).then_inc(list_ready, 1)

            def estep(q, j):
                t = 4 * q + j
                if elive(t - 1):
                    dve.wait_ge(silu_ready, t)
                    wait(dve, ehidT_mm, t - 1)
                    dve.tensor_tensor(hid[:, :], psum[:, 1, I:2 * I], silu_g[:, :], ALU.mult).then_inc(ehid_ready, 1)
                if elive(t - 2):
                    dve.wait_ge(edown_mm, t - 1)
                    wait(dve, y_added, 16 * (t - 3))
                    dve.tensor_scalar(y[:, j % 2, :], bank(3), weight_at[:, bass.ds(t - 2, 1)], None,
                                      ALU.mult).then_inc(y_ready, 1)

            dve.wait_ge(list_ready, 1)
            for i in range(2):
                dve.wait_ge(base_stored[i], 16 * T // 2)
            over_list(dve, estep, 2)

        @block.tensor
        def _(pe):
            pe.wait_ge(ctx_in, 6 * 16)
            pe.wait_ge(const_ready, 3)
            for c in range(C):
                last = pe.matmul(psum[:, c, :].rearrange("p (b k) -> p b k", b=B), wk_sb[:, c * P:(c + 1) * P],
                                 ctx_sb[:, :, 0, :], start=True, stop=True)
            last.then_inc(k_mm, 1)
            for n in range(2):
                pe.matmul(bank(4 + n), ones_row[:, :], bias_rows[:, n, :], start=True, stop=True).then_inc(bias_mm, 1)
            for b in range(B):
                wait(pe, v_copied, 2 * (b - 1))
                pe.matmul(bank(6 + b % 2), ctx_sb[:, b, :, :].rearrange("p d k -> p (d k)"), wv_sb,
                          start=True, stop=True).then_inc(v_mm, 1)

            def transposes(dst, src, n, done):
                for c in range(n):
                    last = pe.transpose(dst[:, c * P:(c + 1) * P], src[:, c * P:(c + 1) * P], ident[:, :])
                last.then_inc(done, 1)

            def product(dst, lhsT, rhs, n, done):
                for c in range(n):
                    last = pe.matmul(dst, lhsT[:, c, :], rhs[c], start=(c == 0), stop=(c == n - 1))
                if done is not None:
                    last.then_inc(done, 1)

            w_gu = [w_sh[:, c * 2 * I:(c + 1) * 2 * I] for c in range(C)]
            w_down = [w_sh[:, GU + c * H:GU + (c + 1) * H] for c in range(CI)]

            def step(b, j):
                tile = TPB * b + j
                t1, t2, t3 = tile - 1, tile - 2, tile - 3
                if live(t2):
                    pe.wait_ge(probs_ready, t2 + 1)
                    wait(pe, x1_ready, t3 + 1)
                    wait(pe, hidT_ready, 2 * (t3))
                    transposes(bank(2, 2), probs[:, :, :].rearrange("p h k -> p (h k)"), PAIRS, probsT_mm)
                if live(t1):
                    pe.wait_ge(qT_ready, t1 + 1)
                    wait(pe, shifted, t1)
                    if isinstance(t1, int) and t1 == 0:
                        pe.wait_ge(kv_copied, 2 + C * HPC)
                    batch = b + (j - 1) // TPB
                    for c in range(C):
                        last = pe.matmul(psum[:, c // 2, (c % 2) * 2 * P:(c % 2) * 2 * P + 2 * P], qT[:, c, :],
                                         k_bd[:, bass.ds(batch, 1), c, :, :].rearrange("p o h k -> p (o h k)"),
                                         start=True, stop=True)
                    last.then_inc(scores_mm, 1)
                if live(t3):
                    pe.wait_ge(xn2_ready, t3 + 1)
                    wait(pe, gu_ready, t3)
                    transposes(bank(4), xn2[:, (j - 3) % 2, :], C, xn2T_mm)
                if live(t2):
                    pe.wait_ge(probsT_ready, t2 + 1)
                    wait(pe, attnT_ready, t2)
                    wait(pe, qT_ready, t1 + 1 if live(t1) else T)
                    if isinstance(t2, int) and t2 == 0:
                        pe.wait_ge(v_copied, 2 * B)
                    batch = b + (j - 2) // TPB
                    for r in range(PAIRS):
                        col = (r % 4) * 2 * VW
                        last = pe.matmul(psum[:, 6 + r // 4, col:col + 2 * VW], probsT[:, r, :],
                                         v_bd[:, bass.ds(batch, 1), r, :, :].rearrange("p o h w -> p (o h w)"),
                                         start=True, stop=True)
                    last.then_inc(av_mm, 1)
                if live(tile):
                    pe.wait_ge(xn1_ready, tile + 1)
                    wait(pe, base_ready, tile - 3)
                    transposes(bank(5), xn1[:, :], C, xn1T_mm)
                if live(t3):
                    pe.wait_ge(xn2T_ready, t3 + 1)
                    if isinstance(t3, int) and t3 == 0:
                        pe.wait_ge(wsh_in, 16)
                    product(bank(4), xn2T, w_gu, C, gu_mm)
                if live(t2):
                    pe.wait_ge(attn_ready, t2 + 1)
                    transposes(bank(6), attn[:, :, :].rearrange("p h d -> p (h d)"), C, attnT_mm)
                if live(tile):
                    pe.wait_ge(xn1T_ready, tile + 1)
                    if isinstance(tile, int) and tile == 0:
                        pe.wait_ge(wq_in, 2 * 16)
                    for o in range(C):
                        for c in range(C):
                            last = pe.matmul(psum[:, 7, o * P:(o + 1) * P], w_q[:, c, o * P:(o + 1) * P],
                                             xn1T[:, c, :], start=(c == 0), stop=(c == C - 1))
                    last.then_inc(q_mm, 1)
                if live(t3):
                    pe.wait_ge(hid_ready, t3 + 1)
                    wait(pe, probsT_ready, t2 + 1 if live(t2) else T)
                    product(psum[:, 3, I:I + E], xn2T, [w_r[:, c, :] for c in range(C)], C, None)
                    transposes(psum[:, 3, :], hid, CI, hidT_mm)
                if live(t2):
                    pe.wait_ge(attnT_ready, t2 + 1)
                    if isinstance(t2, int) and t2 == 0:
                        pe.wait_ge(wo_in, 16)
                    product(bank(2), attnT, [w_o[:, c, :] for c in range(C)], C, proj_mm)
                if live(t3):
                    pe.wait_ge(hidT_ready, 2 * t3 + 1)
                    wait(pe, xn1T_ready, tile + 1 if live(tile) else T)
                    product(bank(5), hidT, w_down, CI, down_mm)

            over_tiles(pe, step, 3)

            pe.wait_ge(both_ready, 1)
            pe.wait_ge(route_const, 3)
            pe.wait_ge(shifted, T)
            pe.matmul(psum[:, 0, 0:TE], tri, both, start=True, stop=True)
            pe.matmul(psum[:, 0, TE:2 * TE], ones_pp, both, start=True, stop=True).then_inc(rank_mm, 1)

            def place(t, k, n, **flags):
                pe.wait_ge(hot_ready, 2 * t + k + 1)
                return pe.matmul(psum[:, 1, 0:2 * SLOTS], hot_lo[:, n, :],
                                 hot_hi[:, n, :, :].rearrange("p v s -> p (v s)"), **flags).then_inc(hot_used, 1)

            for t in range(2):
                for k in range(2):
                    place(t, k, 2 * t + k, start=(t + k == 0), stop=False)
            with pe.Fori(1, T // 2 - 1) as pair:
                for i in range(2):
                    for k in range(2):
                        place(2 * pair + i, k, 2 * i + k, start=False, stop=False)
            for i in range(2):
                for k in range(2):
                    place(T - 2 + i, k, 2 * i + k, start=False, stop=(i + k == 2))

            def expert_weights(e, at, width):
                return w_exp[:, bass.ds(e, 1), at:at + width].rearrange("p o w -> p (o w)")

            def estep(q, j):
                t = 4 * q + j
                if elive(t - 1):
                    pe.wait_ge(xgT_ready, t)
                    wait(pe, ehid_ready, t - 1)
                    plain(pe)
                    e = pe.value_load(expert_of[0:1, bass.ds(t - 1, 1)], min_val=0, max_val=E - 1)
                    product(bank(1), xn2T, [expert_weights(e, c * 2 * I, 2 * I) for c in range(C)], C, egu_mm)
                if elive(t):
                    pe.wait_ge(gathered[j], 16 * (q + 1))
                    wait(pe, xgT_ready, t)
                    transposes(bank(0), x_in[:, j, :], C, xg_mm)
                if elive(t - 2):
                    pe.wait_ge(ehidT_ready, t - 1)
                    wait(pe, y_ready, t - 2)
                    plain(pe)
                    e = pe.value_load(expert_of[0:1, bass.ds(t - 2, 1)], min_val=0, max_val=E - 1)
                    product(bank(3), hidT, [expert_weights(e, GU + c * H, H) for c in range(CI)], CI, edown_mm)
                if elive(t - 1):
                    pe.wait_ge(ehid_ready, t)
                    wait(pe, ehidT_ready, t - 1)
                    transposes(bank(2), hid, CI, ehidT_mm)

            pe.wait_ge(list_ready, 1)
            pe.wait_ge(experts_in, EARLY * 16)
            pe.wait_ge(experts_late_in, (E - EARLY) * 16)
            over_list(pe, estep, 2)


def kernel(**inputs):
    import numpy as np
    import concourse.bacc as bacc
    from concourse.bass_utils import run_bass_kernel_spmd as run

    a = {n: np.asarray(v) for n, v in inputs.items()}

    def rows(w):
        return w.reshape(-1, P, w.shape[-1]).transpose(1, 0, 2)

    def ffn(wg, wu, wd):
        gu = np.concatenate([rows(wg), rows(wu)], axis=2)
        return np.concatenate([gu.reshape(P, -1), rows(wd).reshape(P, -1)], axis=1)

    wg, wu, wd = (a["L0_ffn_" + n] for n in ("wg", "wu", "wd"))
    wkv = a["L0_xattn_Wkv_expand"]
    arrays = {
        "x": a["x"].reshape(TOKENS, H),
        "ctxT": a["ctx_512"].transpose(2, 0, 1),
        "wqT": rows(a["L0_xattn_Wq"].T),
        "wkT": wkv[:H].T,
        "wvT": wkv[H:].T,
        "woT": rows(a["L0_xattn_Wout"].T),
        "routerT": rows(a["L0_ffn_router_w"].T),
        "experts": np.stack([ffn(wg[e], wu[e], wd[e]) for e in range(E)], axis=1),
        "shared": ffn(a["L0_ffn_sg_w"], a["L0_ffn_su_w"], a["L0_ffn_sd_w"]),
        "sh_b": np.concatenate([a["L0_ffn_sg_b"], a["L0_ffn_su_b"]]).reshape(1, 2 * I),
        "sd_b": a["L0_ffn_sd_b"].reshape(1, H),
    }
    arrays = {n: np.ascontiguousarray(v) for n, v in arrays.items()}
    nc = bacc.Bacc("TRN2", target_bir_lowering=False, num_devices=1)
    args = [nc.dram_tensor(n, v.shape, mybir.dt.from_np(v.dtype), kind="ExternalInput").ap() for n, v in arrays.items()]
    out = nc.dram_tensor("out", [TOKENS, H], F32, kind="ExternalOutput").ap()
    xattn_moe(nc, *args, out)
    r = run(nc, [arrays], core_ids=[0])
    return r.results[0]["out"].reshape(B, S, H)
```

```python
import concourse.bass as bass
from concourse import mybir
from contextlib import ExitStack

F32 = mybir.dt.float32
F16 = mybir.dt.float16
I32 = mybir.dt.int32
U32 = mybir.dt.uint32
ALU = mybir.AluOpType
ACT = mybir.ActivationFunctionType
AX = mybir.AxisListType

P = 128
B, S, H = 8, 512, 512
NH, HD = 16, 32
SK, L = 64, 128
E, I = 8, 256
C = H // P
CI = I // P
PAIRS = NH // 2
HPC = P // HD
TPB = S // P
T = B * S // P
TOKENS = T * P
SLOTS = 2 * T + E - 1
VW = HD + 1
ROW = H + E
EPS = 1e-5
BIG = 3.4e38
FAR = 8192.0
TINY = 2.0 ** -50
SCALE = float(HD) ** -0.5
GU = C * 2 * I
WE = GU + CI * H
PIECE = 512
PIECES = WE // PIECE

W_UP = 2.0 ** 14
X_UP = 2.0 ** 11
P_UP = 2.0 ** 14
KV_UP = 2.0 ** 6
Q_DOWN = 2.0 ** -20
XW = 1.0 / (X_UP * W_UP)

M_CTX, M_WK, M_WV, M_WQ, M_WO, M_GU, M_DOWN, M_BIAS, M_R = range(9)
N_MAG = 9
MAGS = N_MAG - M_WO
(S_K, S_V, S_EXP, S_X1, S_GU, S_HID, S_BASE, S_R, S_TMP, S_TMP2) = range(10)
N_SC = 10


def xattn_moe(nc, x, ctxT, wqT, wkT, wvT, woT, routerT, experts, shared, sh_b, sd_b, out):
    xn_dram = nc.dram_tensor("normed_tokens", [TOKENS, ROW], F32, kind="Internal").ap()
    mag_dram = nc.dram_tensor("magnitudes", [E * P * 3], F32, kind="Internal").ap()
    stack = ExitStack()
    with stack:
        def sb(name, shape, dt=F32):
            return stack.enter_context(nc.sbuf_tensor(name, shape, dt))

        def sem(name):
            return stack.enter_context(nc.semaphore(name))

        exp_all = sb("exp_all", [P, WE // 2 + E * WE])
        exp_raw = exp_all[:, WE // 2:]
        w_exp = exp_all[:, 0:E * WE].bitcast(F16).rearrange("p (e v w) -> p e v w", e=E, v=2)
        stage = exp_all[:, 4 * WE:]
        at = 0
        staged = []
        for n in (B * 2 * SK, 512, 512, C * H, C * H, WE, C * E):
            staged.append(stage[:, at:at + n])
            at += n
        ctx_sb, wk_sb, wv_sb, wq_raw, wo_raw, sh_raw, r_raw = staged
        ctx_sb = ctx_sb.rearrange("p (b d k) -> p b d k", b=B, d=2)
        w_sh = sb("w_sh", [P, 2, WE], F16)
        w_q = sb("w_q", [P, 2, C * H], F16)
        w_o = sb("w_o", [P, 2, C * H], F16)
        w_r = sb("w_r", [P, 2, C * E], F16)
        sizes = (C * B * SK, B * PAIRS * HD, C * HPC * SK, PAIRS * 2 * VW)
        kv_store = sb("kv_store", [P, sum(sizes)])[:, :]
        k_all, v_all, k_bd, v_bd = [kv_store[:, sum(sizes[:n]):sum(sizes[:n + 1])].bitcast(F16) for n in range(4)]
        k_all = k_all.rearrange("p (v c k) -> p v c k", v=2, c=C)
        v_all = v_all.rearrange("p (v b r d) -> p v b r d", v=2, b=B, r=PAIRS)
        k_bd = k_bd.rearrange("p (v c h k) -> p v c h k", v=2, c=C, h=HPC)
        v_bd = v_bd.rearrange("p (v r h w) -> p v r h w", v=2, r=PAIRS, h=2)
        bd_flat = kv_store[:, sum(sizes[:2]):]
        ident = sb("ident", [P, P])
        sh_bias = sb("sh_bias", [P, 2 * I])
        sd_bias = sb("sd_bias", [P, H])
        mask = sb("mask", [P, SK])
        minus_half = sb("minus_half", [P, 1])
        mags = sb("mags", [P, N_MAG])
        maxima = sb("maxima", [P, N_MAG])
        mag_max = sb("mag_max", [MAGS, 2])
        mag_diag = sb("mag_diag", [MAGS, 2, MAGS])
        ones_rows = sb("ones_rows", [MAGS, P])
        pow2 = sb("pow2", [P, N_MAG])
        inv2 = sb("inv2", [P, N_MAG])
        sc = sb("sc", [P, N_SC])
        emag = sb("emag", [P, 3])
        emax = sb("emax", [P, 3])
        epow = sb("epow", [P, E, 2])
        einv = sb("einv", [P, E, 2])
        esc = sb("esc", [P, E, 2])
        x_in = sb("x_in", [P, 4, ROW])
        xn1 = sb("xn1", [P, H])
        xn1T = sb("xn1T", [P, 2, C, P], F16)
        qT = sb("qT", [P, 2, C, P], F16)
        probs = sb("probs", [P, NH, SK])
        probsT = sb("probsT", [P, 2, PAIRS, P], F16)
        attn = sb("attn", [P, NH, HD])
        attnT = sb("attnT", [P, 2, C, P], F16)
        xy = sb("xy", [P, 2, H])
        x1, base = xy[:, 0, :], xy[:, 1, :]
        xn2 = sb("xn2", [P, 2, ROW])
        xn2T = sb("xn2T", [P, 2, C, P], F16)
        gate_up = sb("gate_up", [P, 2 * I])
        hid = sb("hid", [P, I])
        hidT = sb("hidT", [P, 2, CI, P], F16)
        piece = sb("piece", [P, PIECE])
        mag_rows = sb("mag_rows", [P, P * 3])
        stats = sb("stats", [P, 2, 6])
        moments = sb("moments", [P, 2, 2])
        rstd = sb("rstd", [P, 2, 3])
        recip = sb("recip", [P, NH])
        head_max = sb("head_max", [P, NH])
        logits = sb("logits", [P, T, E])
        TE = T * E

        def scratch(n):
            return kv_store[:, n * TE:(n + 1) * TE]

        (eq, oneh1, oneh2, second, both, totals, ones_te, cum, before, rank_all, selected,
         steps128, rev) = [scratch(n) for n in range(13)]
        te = dict(t=T, e=E)
        xn2_flat = xn2[:, :, :].rearrange("p a h -> p (a h)")
        x_flat = x_in[:, :, :].rearrange("p a h -> p (a h)")
        small = x_flat[:, 0:8 * T]
        picked = x_flat[:, 256:256 + 12 * T].rearrange("p (n k t) -> p n k t", n=6, k=2)
        picked_i = x_flat[:, 640:640 + 4 * T].bitcast(I32).rearrange("p (n k t) -> p n k t", n=2, k=2)
        SE = SLOTS * E
        se_tab = x_flat[:, 768:768 + SE].rearrange("p (s e) -> p s e", e=E)
        iota_e = x_flat[:, 1360:1360 + E]
        e_scales = x_flat[:, 1368:1368 + 3 * E].rearrange("p (n e) -> p n e", n=3)
        tri = xn1[:, 0:P]
        ones_pp = xn1[:, P:2 * P]
        iota_p = xn1[:, 2 * P:3 * P]
        iota_s = xn1[:, 3 * P:3 * P + SLOTS]
        token_no = small[:, 0:T]
        probs_flat = probs[:, :, :].rearrange("p h k -> p (h k)")
        hot_lo = probs_flat[:, 0:4 * P].bitcast(F16).rearrange("p (n q) -> p n q", n=8)
        hot_hi = probsT[:, :, :, :].rearrange("p v r q -> p (v r q)")[:, 0:8 * SLOTS].rearrange("p (n s) -> p n s", n=8)
        y_scale_at = xn2_flat[:, 0:SE].rearrange("p (s e) -> p s e", e=E)
        at_tabs = [gate_up[:, n * SLOTS:(n + 1) * SLOTS] for n in range(4)]
        gate_scale_at, up_scale_at = at_tabs[0:2]
        gather_at, add_at = [a.bitcast(U32) for a in at_tabs[2:4]]
        expert_of = sb("expert_of", [1, SLOTS], I32)
        gather_now = sb("gather_now", [P, 4], U32)
        add_now = sb("add_now", [P, 2], U32)
        y = xy
        attn_flat = attn[:, :, :].rearrange("p h d -> p (h d)")
        silu_g = attn_flat[:, 0:I]
        y_w = sb("y_w", [P, 2, 1])
        y_w_terms = sb("y_w_terms", [P, E])

        psum = stack.enter_context(nc.psum_tensor("psum", [P, 8, 512], F32))

        def bank(n, k=1):
            return psum[:, n:n + k, :].rearrange("p n w -> p (n w)")

        def flat(t4):
            return t4.rearrange("p c q -> p (c q)")

        waits_met = sem("waits_met")
        ctx_in, wq_in, wo_in, wsh_in, bias_in = [sem(n) for n in ("ctx_in", "wq_in", "wo_in", "wsh_in", "bias_in")]
        const_made, const_ready, kv_zeroed = sem("const_made"), sem("const_ready"), sem("kv_zeroed")
        mags_ready, mags_turned, diag_ready, mags_spread, scale_chain, scales_ready = [sem(n) for n in (
            "mags_ready", "mags_turned", "diag_ready", "mags_spread", "scale_chain", "scales_ready")]
        wq_hi, wq_split, wo_hi, wo_split, wsh_hi, wsh_scaled, wsh_split = [sem(n) for n in (
            "wq_hi", "wq_split", "wo_hi", "wo_split", "wsh_hi", "wsh_scaled", "wsh_split")]
        k_mm, k_hi, k_split, v_mm, v_hi, v_split, k_bd_ready, v_bd_ready = [sem(n) for n in (
            "k_mm", "k_hi", "k_split", "v_mm", "v_hi", "v_split", "k_bd_ready", "v_bd_ready")]
        expert_in, e_mags, e_mags_stored, e_mags_back, e_chain, e_scales_ready, piece_hi, piece_split = [
            sem(n) for n in ("expert_in", "e_mags", "e_mags_stored", "e_mags_back", "e_chain", "e_scales_ready",
                             "piece_hi", "piece_split")]
        x_loaded = [sem(f"x_loaded{i}") for i in range(4)]
        ln_chain = [sem("ln1_chain"), sem("ln2_chain")]
        ln_var = [sem("ln1_var"), sem("ln2_var")]
        ln_eps = [sem("ln1_eps"), sem("ln2_eps")]
        ln_pow = [sem("ln1_pow"), sem("ln2_pow")]
        ln_rstd = [sem("ln1_rstd"), sem("ln2_rstd")]
        xn1_ready, xn1T_mm, xn1T_hi, xn1T_ready, q_mm, qT_hi, qT_ready = [sem(n) for n in (
            "xn1_ready", "xn1T_mm", "xn1T_hi", "xn1T_ready", "q_mm", "qT_hi", "qT_ready")]
        scores_mm, masked, max_ready, shifted, probs_ready = [sem(n) for n in (
            "scores_mm", "masked", "max_ready", "shifted", "probs_ready")]
        probsT_mm, probsT_hi, probsT_ready, av_mm, recip_ready, attn_ready = [sem(n) for n in (
            "probsT_mm", "probsT_hi", "probsT_ready", "av_mm", "recip_ready", "attn_ready")]
        attnT_mm, attnT_hi, attnT_ready, proj_mm, x1_ready, x1b_ready = [sem(n) for n in (
            "attnT_mm", "attnT_hi", "attnT_ready", "proj_mm", "x1_ready", "x1b_ready")]
        xn2_ready, xn2T_mm, xn2T_hi, xn2T_ready, gu_mm, gu_ready, gu_prod, tanh_ready = [sem(n) for n in (
            "xn2_ready", "xn2T_mm", "xn2T_hi", "xn2T_ready", "gu_mm", "gu_ready", "gu_prod", "tanh_ready")]
        hid_ready, hidT_mm, hidT_hi, logits_ready, hidT_ready, down_mm, base_ready, base_stored = [sem(n) for n in (
            "hid_ready", "hidT_mm", "hidT_hi", "logits_ready", "hidT_ready", "down_mm", "base_ready", "base_stored")]
        xn2_stored = [sem(f"xn2_stored{i}") for i in range(2)]
        route_const, route_chain, both_ready, rank_mm = [sem(n) for n in (
            "route_const", "route_chain", "both_ready", "rank_mm")]
        places_ready, hot_hi_ready, hot_lo0_ready, hot_lo1_ready, hot_used, list_ready = [sem(n) for n in (
            "places_ready", "hot_hi_ready", "hot_lo0_ready", "hot_lo1_ready", "hot_used", "list_ready")]
        lo_set = sem("lo_set")
        gather_set, add_set = sem("gather_set"), sem("add_set")
        gathered = [sem(f"gathered{i}") for i in range(4)]
        xg_mm, xgT_hi, xgT_ready, egu_mm, silu_ready, ehid_ready, ehidT_mm, ehidT_hi, ehidT_ready = [sem(n) for n in (
            "xg_mm", "xgT_hi", "xgT_ready", "egu_mm", "silu_ready", "ehid_ready", "ehidT_mm", "ehidT_hi",
            "ehidT_ready")]
        edown_mm, y_w_made, y_w_ready, y_ready, y_added = [sem(n) for n in (
            "edown_mm", "y_w_made", "y_w_ready", "y_ready", "y_added")]

        def live(tile):
            return not isinstance(tile, int) or 0 <= tile < T

        def wait(eng, semaphore, value):
            if not isinstance(value, int) or value > 0:
                eng.wait_ge(semaphore, value)

        def plain(eng):
            eng.sem_inc(waits_met, 1)

        def over_tiles(eng, step, behind):
            for b in range(2):
                for j in range(TPB):
                    step(b, j)
            with eng.Fori(2, B) as b:
                for j in range(TPB):
                    step(b, j)
            for j in range(behind):
                step(B + j // TPB, j % TPB)

        def elive(tile):
            return not isinstance(tile, int) or 0 <= tile < SLOTS

        def over_list(eng, step, behind):
            for j in range(4):
                step(0, j)
            with eng.Fori(1, SLOTS // 4) as q:
                for j in range(4):
                    step(q, j)
            for j in range(SLOTS % 4 + behind):
                step(SLOTS // 4 + j // 4, j % 4)

        def found(e):
            return None if isinstance(e, int) and not 0 <= e < E else e

        def pieces_at(b, j):
            e = found(b - 1)
            return (None, ()) if e is None else (e, ((0,), (1, 2), (3,), (4, 5))[j])

        def raw_piece(e, k):
            return exp_raw[:, bass.ds(e * WE + k * PIECE, PIECE)]

        def split_piece(e, v, k):
            return w_exp[:, bass.ds(e, 1), v, k * PIECE:(k + 1) * PIECE].rearrange("p o w -> p (o w)")

        def value_parts(v, b, h):
            rows = slice(SK * h, SK * h + SK)
            at = (4 + b) % 8
            return v_all[rows, v, b:b + 4, :, :], psum[rows, at:at + 4, :].rearrange(
                "p b (r h d) -> p b r h d", h=2, d=HD)[:, :, :, h, :]

        block = stack.enter_context(nc.Block())

        @block.sync
        def _(sp):
            def load_x(b, j):
                tile = TPB * b + j
                wait(sp, x1_ready, tile - 3)
                sp.dma_start(x_in[:, j, 0:H], x[bass.ds(tile * P, P), :]).then_inc(x_loaded[j], 16)

            def load_expert(e):
                sp.dma_start(exp_raw[:, bass.ds(e * WE, WE)],
                             experts[:, bass.ds(e, 1), :].rearrange("p o w -> p (o w)")).then_inc(expert_in, 16)

            def through_dram(e):
                here = mag_dram[bass.ds(e * P * 3, P * 3)]
                sp.wait_ge(e_mags, 3 * (e + 1))
                sp.dma_start(here.rearrange("(p n) -> p n", n=3), emag[:, :]).then_inc(e_mags_stored, 16)
                sp.wait_ge(e_mags_stored, 16 * (e + 1))
                sp.dma_start(mag_rows[:, :], here.partition_broadcast(P)).then_inc(e_mags_back, 16)

            def step(b, j):
                tile = TPB * b + j
                t4 = tile - 4
                if live(tile + 1) and not (isinstance(b, int) and (b, j) == (0, 0)):
                    load_x(*((b, j + 1) if j < 3 else (b + 1, 0)))
                if live(t4):
                    sp.wait_ge(logits_ready, 2 * (t4 + 1))
                    sp.dma_start(xn_dram[bass.ds(t4 * P, P), :], xn2[:, j % 2, :]).then_inc(xn2_stored[j % 2], 16)
                e = found(b + 1)
                if j == 0 and isinstance(b, int) and b == 2:
                    sp.wait_ge(wsh_split, 3)
                    sp.wait_ge(wo_split, 1)
                    sp.wait_ge(wq_split, 1)
                    sp.wait_ge(k_split, 1)
                    sp.wait_ge(v_split, 4)
                if j == 0 and e is not None:
                    sp.wait_ge(expert_in, 16 * e)
                    load_expert(e)
                if live(t4):
                    sp.wait_ge(base_ready, t4 + 1)
                    sp.dma_start(out[bass.ds(t4 * P, P), :], base).then_inc(base_stored, 16)
                if j == 2 and found(b) is not None:
                    through_dram(b)

            load_x(0, 0)
            sp.dma_start(wk_sb, wkT).then_inc(ctx_in, 16)
            for d in range(2):
                sp.dma_start(ctx_sb[:, :, d, :], ctxT).then_inc(ctx_in, 16)
            sp.dma_start(wv_sb, wvT).then_inc(ctx_in, 16)
            sp.dma_start(wq_raw, wqT).then_inc(wq_in, 16)
            load_x(0, 1)
            sp.dma_start(wo_raw, woT).then_inc(wo_in, 16)
            sp.dma_start(r_raw, routerT).then_inc(wsh_in, 16)
            sp.dma_start(sh_raw, shared).then_inc(wsh_in, 16)
            sp.dma_start(sh_bias[:, :], sh_b.partition_broadcast(P)).then_inc(bias_in, 16)
            sp.dma_start(sd_bias[:, :], sd_b.partition_broadcast(P)).then_inc(bias_in, 16)
            load_expert(0)
            for b in range(3):
                for j in range(TPB):
                    step(b, j)
            with sp.Fori(3, B - 1) as b:
                for j in range(TPB):
                    step(b, j)
            for j in range(TPB):
                step(B - 1, j)
            for j in range(4):
                step(B, j)

        @block.gpsimd
        def _(pool):
            pool.memset(ident[:, :], 0.0).then_inc(const_made, 1)
            pool.memset(mask[:, :], BIG).then_inc(const_made, 1)
            pool.memset(minus_half[:, :], -0.5).then_inc(const_made, 1)
            pool.wait_ge(const_made, 3)
            pool.affine_select(out=ident[:, :], in_=ident[:, :], compare_op=ALU.not_equal, fill=1.0, base=0,
                               pattern=[[-1, P]], channel_multiplier=1).then_inc(const_ready, 1)
            pool.affine_select(out=mask[:, :], in_=mask[:, :], compare_op=ALU.is_ge, fill=-BIG, base=0,
                               pattern=[[-1, SK]], channel_multiplier=1).then_inc(const_ready, 1)
            pool.memset(ones_rows[:, :], 1.0).then_inc(const_ready, 1)
            pool.memset(bd_flat, 0.0).then_inc(kv_zeroed, 1)
            pool.wait_ge(kv_zeroed, 1)
            pool.wait_ge(const_ready, 3)
            for h in range(2):
                pool.memset(v_bd[SK * h:SK * h + SK, 0, :, h, HD:VW], 1.0).then_inc(kv_zeroed, 1)
            pool.wait_ge(kv_zeroed, 3)

            def inv_std(which, tile):
                pool.wait_ge(ln_var[which], tile + 1)
                plain(pool)
                pool.tensor_scalar(rstd[:, which, 0:1], moments[:, which, 1:2], EPS, None, ALU.add).then_inc(ln_eps[which], 1)
                pool.wait_ge(ln_eps[which], tile + 1)
                pool.tensor_tensor(rstd[:, which, 1:2], rstd[:, which, 0:1], minus_half[:, :],
                                   ALU.pow).then_inc(ln_pow[which], 1)
                pool.wait_ge(ln_pow[which], tile + 1)
                plain(pool)
                pool.tensor_scalar(rstd[:, which, 2:3], moments[:, which, 0:1], -1.0, rstd[:, which, 1:2],
                                   ALU.mult, ALU.mult).then_inc(ln_rstd[which], 1)

            def low_piece(e, k):
                pool.wait_ge(piece_hi, 2 * (e * PIECES + k + 1))
                plain(pool)
                pool.tensor_tensor(split_piece(e, 1, k), piece[:, :], split_piece(e, 0, k),
                                   ALU.subtract).then_inc(piece_split, 1)

            def step(b, j):
                tile = TPB * b + j
                t3 = tile - 3
                e, pieces = pieces_at(b, j)
                if live(t3):
                    inv_std(1, t3)
                if live(tile):
                    inv_std(0, tile)
                if pieces:
                    low_piece(e, pieces[0])
                if live(t3):
                    pool.wait_ge(gu_ready, t3 + 1)
                    pool.tensor_tensor(gate_up[:, I:2 * I], gate_up[:, 0:I], gate_up[:, I:2 * I], ALU.mult).then_inc(gu_prod, 1)
                    wait(pool, base_stored, 16 * t3)
                    if isinstance(t3, int) and t3 == 0:
                        pool.wait_ge(bias_in, 32)
                    pool.tensor_tensor(base, x1, sd_bias[:, :], ALU.add).then_inc(x1b_ready, 1)
                if len(pieces) > 1:
                    low_piece(e, pieces[1])
                if isinstance(b, int) and (b, j) == (0, 1):
                    for n, (a, z) in enumerate(((0, GU), (GU, WE))):
                        pool.wait_ge(wsh_scaled, n + 1)
                        pool.tensor_tensor(w_sh[:, 1, a:z], sh_raw[:, a:z], w_sh[:, 0, a:z], ALU.subtract).then_inc(wsh_split, 1)

            over_tiles(pool, step, 4)

            pool.wait_ge(av_mm, T)
            pool.wait_ge(xn1T_mm, T)
            pool.wait_ge(x1_ready, T)
            pool.memset(tri, 1.0).then_inc(route_const, 1)
            pool.memset(ones_pp, 1.0).then_inc(route_const, 1)
            pool.wait_ge(route_const, 1)
            pool.affine_select(out=tri, in_=tri, compare_op=ALU.is_ge, fill=0.0, base=-1,
                               pattern=[[1, P]], channel_multiplier=-1).then_inc(route_const, 1)

            def iota(dst, pattern, base_value, per_partition):
                pool.iota(dst, pattern=pattern, base=base_value, channel_multiplier=per_partition,
                          allow_small_or_imprecise_dtypes=True).then_inc(route_const, 1)

            iota(rev.rearrange("p (t e) -> p t e", **te), [[0, T], [-1, E]], E, 0)
            iota(steps128.rearrange("p (e t) -> p e t", **te), [[0, E], [P, T]], 0, 0)
            iota(iota_p, [[1, P]], 0, 0)
            iota(iota_s, [[1, SLOTS]], 0, 0)
            iota(iota_e, [[1, E]], 0, 0)
            iota(token_no.rearrange("p (h t) -> p h t", h=2), [[0, 2], [P, T // 2]], 1, 1)

            lo_places = picked[:, 3, 1, :]

            lo_now = small[:, T:T + 4]

            def hot_lows(quad):
                if not isinstance(quad, int):
                    pool.wait_ge(hot_lo1_ready, 4 * quad)
                    plain(pool)
                pool.tensor_copy(lo_now, lo_places[:, bass.ds(4 * quad, 4)]).then_inc(lo_set, 1)
                pool.wait_ge(lo_set, quad + 1)
                for i in range(4):
                    if not isinstance(quad, int):
                        pool.wait_ge(hot_used, 8 * quad + (2 * i - 6))
                    plain(pool)
                    pool.tensor_scalar(hot_lo[:, 2 * i + 1, :], iota_p, lo_now[:, i:i + 1], None, ALU.is_equal
                                       ).then_inc(hot_lo1_ready, 1)

            pool.wait_ge(places_ready, 1)
            hot_lows(0)
            with pool.Fori(1, T // 4) as quad:
                hot_lows(quad)

            pool.wait_ge(list_ready, 1)
            for i in range(2):
                pool.wait_ge(xn2_stored[i], 16 * T // 2)
            pool.wait_ge(base_stored, 16 * T)

            def gather(tile, ring):
                wait(pool, y_w_ready, tile - 3)
                plain(pool)
                pool.tensor_copy(gather_now[:, ring:ring + 1], gather_at[:, bass.ds(tile, 1)]).then_inc(gather_set, 1)
                pool.wait_ge(gather_set, tile + 1)
                plain(pool)
                pool.indirect_dma_start(x_in[:, ring, :], None, xn_dram,
                                        bass.IndirectOffsetOnAxis(gather_now[:, ring:ring + 1], 0)
                                        ).then_inc(gathered[ring], 16)

            def add(tile, ring):
                plain(pool)
                pool.tensor_copy(add_now[:, ring:ring + 1], add_at[:, bass.ds(tile, 1)]).then_inc(add_set, 1)
                pool.wait_ge(add_set, tile + 1)
                pool.wait_ge(y_ready, tile + 1)
                wait(pool, y_added, 16 * tile)
                plain(pool)
                pool.indirect_dma_start(out, bass.IndirectOffsetOnAxis(add_now[:, ring:ring + 1], 0),
                                        y[:, ring, :], None, bounds_check=TOKENS - 1, oob_is_err=False,
                                        compute_op=ALU.add).then_inc(y_added, 16)

            for t in range(8):
                gather(t, t % 4)
                if t >= 6:
                    add(t - 6, t % 2)
            with pool.Fori(2, SLOTS // 4) as q:
                for j in range(4):
                    gather(4 * q + j, j)
                    add(4 * q + (j - 6), j % 2)
            for t in range(SLOTS // 4 * 4, SLOTS + 6):
                if t < SLOTS:
                    gather(t, t % 4)
                add(t - 6, t % 2)
            pool.wait_ge(y_added, 16 * SLOTS)

        @block.scalar
        def _(act):
            def copy(dst, src, scale, done):
                act.activation(dst, src, ACT.Copy, scale=scale).then_inc(done, 1)

            def first_weights():
                act.wait_ge(scales_ready, 1)
                act.wait_ge(k_mm, 1)
                copy(k_all[:, 0, :, :].rearrange("p c k -> p (c k)"), bank(0, 4), sc[:, S_K:S_K + 1], k_hi)
                copy(w_q[:, 0, :], wq_raw, sc[:, S_TMP:S_TMP + 1], wq_hi)
                for b in (0, 4):
                    act.wait_ge(v_mm, b + 4)
                    for h in range(2):
                        copy(*value_parts(0, b, h), sc[SK * h:SK * h + SK, S_V:S_V + 1], v_hi)

            def more_weights():
                act.wait_ge(wo_in, 16)
                act.wait_ge(wsh_in, 32)
                act.wait_ge(scales_ready, 2)
                copy(w_o[:, 0, :], wo_raw, inv2[:, M_WO:M_WO + 1], wo_hi)
                copy(w_sh[:, 0, 0:GU], sh_raw[:, 0:GU], inv2[:, M_GU:M_GU + 1], wsh_hi)
                copy(w_sh[:, 0, GU:WE], sh_raw[:, GU:WE], inv2[:, M_DOWN:M_DOWN + 1], wsh_hi)
                copy(w_r[:, 0, :], r_raw, inv2[:, M_R:M_R + 1], wsh_hi)
                for n, (a, z, m) in enumerate(((0, GU, M_GU), (GU, WE, M_DOWN))):
                    act.wait_ge(wsh_hi, n + 1)
                    copy(sh_raw[:, a:z], sh_raw[:, a:z], inv2[:, m:m + 1], wsh_scaled)

            def batch_keys(b):
                for h in range(HPC):
                    rows = slice(HD * h, HD * h + HD)
                    plain(act)
                    copy(k_bd[rows, :, :, h, :], k_all[rows, :, :, bass.ds(b * SK, SK)], 1.0, k_bd_ready)

            def high_piece(e, k):
                which = 0 if k < GU // PIECE else 1
                esc_now = esc[:, bass.ds(e, 1), which]
                act.wait_ge(e_scales_ready, e + 1)
                wait(act, piece_split, e * PIECES + k)
                plain(act)
                copy(split_piece(e, 0, k), raw_piece(e, k), esc_now, piece_hi)
                copy(piece[:, :], raw_piece(e, k), esc_now, piece_hi)

            def step(b, j):
                tile = TPB * b + j
                t1, t2, t3, t4 = [tile - n for n in range(1, 5)]
                e, pieces = pieces_at(b, j)
                first = isinstance(b, int) and (b, j) == (0, 0)
                if live(t4):
                    act.wait_ge(hidT_mm, t4 + 1)
                    copy(flat(hidT[:, 0, :, :]), psum[:, 4, 0:I], sc[:, S_HID:S_HID + 1], hidT_hi)
                    copy(logits[:, bass.ds(t4, 1), :], psum[:, 4, I:I + E], sc[:, S_R:S_R + 1], logits_ready)
                    copy(xn2[:, j % 2, H:ROW], psum[:, 4, I:I + E], sc[:, S_R:S_R + 1], logits_ready)
                if live(t2):
                    act.wait_ge(probsT_mm, t2 + 1)
                    for n in range(2):
                        copy(probsT[:, 0, 4 * n:4 * n + 4, :], bank(n), P_UP, probsT_hi)
                if live(t3):
                    act.wait_ge(ln_rstd[1], t3 + 1)
                    wait(act, xn2_stored[(j + 1) % 2], 16 * (TPB // 2 * b + (j - 3) // 2))
                    act.activation(xn2[:, (j + 1) % 2, 0:H], x1, ACT.Identity, bias=rstd[:, 1, 2:3],
                                   scale=rstd[:, 1, 1:2]).then_inc(xn2_ready, 1)
                if live(t1):
                    act.wait_ge(q_mm, t1 + 1)
                    copy(flat(qT[:, 0, :, :]), bank(5), Q_DOWN, qT_hi)
                if pieces:
                    high_piece(e, pieces[0])
                if live(t3):
                    act.wait_ge(xn2T_mm, t3 + 1)
                    copy(flat(xn2T[:, 0, :, :]), bank(6), X_UP, xn2T_hi)
                if j == 1 and live(tile):
                    wait(act, av_mm, tile - 1)
                    if isinstance(b, int) and b == 0:
                        act.wait_ge(v_split, 4)
                    for h in range(2):
                        rows = slice(SK * h, SK * h + SK)
                        plain(act)
                        copy(v_bd[rows, :, :, h, 0:HD],
                             v_all[rows, :, bass.ds(b, 1), :, :].rearrange("p v o r d -> p v (o r) d"), 1.0, v_bd_ready)
                if live(tile):
                    act.wait_ge(ln_rstd[0], tile + 1)
                    act.activation(xn1[:, :], x_in[:, j, 0:H], ACT.Identity, bias=rstd[:, 0, 2:3],
                                   scale=rstd[:, 0, 1:2]).then_inc(xn1_ready, 1)
                if live(t2):
                    act.wait_ge(attnT_mm, t2 + 1)
                    copy(flat(attnT[:, 0, :, :]), bank(4), 1.0, attnT_hi)
                if j == 0 and live(tile) and not first:
                    act.wait_ge(scores_mm, tile)
                    batch_keys(b)
                if len(pieces) > 1:
                    high_piece(e, pieces[1])
                if live(t1):
                    act.wait_ge(shifted, t1 + 1)
                    act.activation(probs[:, :, :], probs[:, :, :], ACT.Exp, scale=sc[:, S_EXP:S_EXP + 1]).then_inc(probs_ready, 1)
                if live(tile):
                    act.wait_ge(xn1T_mm, tile + 1)
                    copy(flat(xn1T[:, 0, :, :]), bank(7), X_UP, xn1T_hi)
                if live(t3):
                    act.wait_ge(gu_ready, t3 + 1)
                    act.activation(hid[:, :], gate_up[:, 0:I], ACT.Tanh, scale=0.5).then_inc(tanh_ready, 1)
                if first:
                    first_weights()
                    act.wait_ge(k_split, 1)
                    batch_keys(0)
                if isinstance(b, int) and (b, j) == (0, 1):
                    more_weights()

            over_tiles(act, step, 4)

            def estep(q, j):
                t = 4 * q + j
                if elive(t - 2):
                    act.wait_ge(ehidT_mm, t - 1)
                    copy(flat(hidT[:, 0, :, :]), psum[:, 2, 0:I], 1.0, ehidT_hi)
                if elive(t - 1):
                    act.wait_ge(egu_mm, t)
                    plain(act)
                    act.activation(silu_g, psum[:, 1, 0:I], ACT.Silu, scale=gate_scale_at[:, bass.ds(t - 1, 1)]
                                   ).then_inc(silu_ready, 1)
                if elive(t):
                    act.wait_ge(xg_mm, t + 1)
                    copy(flat(xn2T[:, 0, :, :]), bank(0), X_UP, xgT_hi)

            act.wait_ge(list_ready, 1)
            over_list(act, estep, 2)

        @block.vector
        def _(dve):
            links = [0]

            def link(ins):
                links[0] += 1
                ins.then_inc(scale_chain, 1)
                dve.wait_ge(scale_chain, links[0])

            def magnitude(col, src):
                dve.tensor_reduce(mags[:, col:col + 1], src, AX.X, ALU.max, apply_absolute_value=True).then_inc(mags_ready, 1)

            def powers(a, z, group):
                n = z - a
                dve.wait_ge(mags_turned, group)
                link(dve.tensor_reduce(mag_max[0:n, group - 1:group], psum[0:n, 6, 0:P], AX.X, ALU.max))
                dve.tensor_scalar(mag_diag[0:n, group - 1, 0:n], ident[0:n, 0:n], mag_max[0:n, group - 1:group], None,
                                  ALU.mult).then_inc(diag_ready, 1)
                dve.wait_ge(mags_spread, group)
                link(dve.tensor_scalar(maxima[:, a:z], psum[:, 6, P:P + n], TINY, None, ALU.max))
                link(dve.tensor_scalar(pow2[:, a:z].bitcast(I32), maxima[:, a:z].bitcast(I32), 0x7F800000, None,
                                       ALU.bitwise_and))
                link(dve.tensor_scalar(inv2[:, a:z].bitcast(I32), pow2[:, a:z].bitcast(I32), -1.0, float(0x7F000000),
                                       ALU.mult, ALU.add))

            def col(table, n):
                return table[:, n:n + 1]

            def low(dst, src, scale, high, done):
                dve.scalar_tensor_tensor(dst, src, scale, high, ALU.mult, ALU.subtract).then_inc(done, 1)

            def first_weights():
                dve.wait_ge(ctx_in, 64)
                magnitude(M_CTX, staged[0])
                magnitude(M_WK, wk_sb)
                magnitude(M_WV, wv_sb)
                dve.wait_ge(wq_in, 16)
                magnitude(M_WQ, wq_raw)
                powers(0, M_WO, 1)
                link(dve.tensor_scalar(col(sc, S_TMP), col(inv2, M_WQ), W_UP, None, ALU.mult))
                link(dve.tensor_scalar(col(sc, S_K), col(inv2, M_WK), col(inv2, M_CTX), KV_UP, ALU.mult, ALU.mult))
                link(dve.tensor_scalar(col(sc, S_V), col(inv2, M_WV), col(inv2, M_CTX), KV_UP, ALU.mult, ALU.mult))
                link(dve.tensor_scalar(col(sc, S_EXP), col(pow2, M_WK), col(pow2, M_CTX), SCALE * XW / (Q_DOWN * KV_UP),
                                       ALU.mult, ALU.mult))
                dve.tensor_scalar(col(sc, S_EXP), col(sc, S_EXP), col(pow2, M_WQ), None, ALU.mult).then_inc(scales_ready, 1)
                dve.wait_ge(k_hi, 1)
                low(k_all[:, 1, :, :].rearrange("p c k -> p (c k)"), bank(0, 4), col(sc, S_K),
                    k_all[:, 0, :, :].rearrange("p c k -> p (c k)"), k_split)
                for n, b in enumerate((0, 4)):
                    for h in range(2):
                        dve.wait_ge(v_hi, 2 * n + h + 1)
                        dst, src = value_parts(1, b, h)
                        low(dst, src, sc[SK * h:SK * h + SK, S_V:S_V + 1], value_parts(0, b, h)[0], v_split)
                    if n == 0:
                        dve.wait_ge(wq_hi, 1)
                        low(w_q[:, 1, :], wq_raw, col(sc, S_TMP), w_q[:, 0, :], wq_split)
                dve.wait_ge(wo_in, 16)
                magnitude(M_WO, wo_raw)
                dve.wait_ge(wsh_in, 32)
                magnitude(M_GU, sh_raw[:, 0:GU])
                magnitude(M_DOWN, sh_raw[:, GU:WE])
                dve.wait_ge(bias_in, 32)
                magnitude(M_BIAS, sh_bias[:, :])
                magnitude(M_R, r_raw)

            def more_scales():
                powers(M_WO, N_MAG, 2)
                link(dve.tensor_scalar(col(sc, S_X1), col(pow2, M_WV), col(pow2, M_CTX), 1.0 / (KV_UP * W_UP),
                                       ALU.mult, ALU.mult))
                link(dve.tensor_scalar(col(sc, S_X1), col(sc, S_X1), col(pow2, M_WO), None, ALU.mult))
                link(dve.tensor_scalar(col(sc, S_GU), col(pow2, M_GU), XW, None, ALU.mult))
                link(dve.tensor_scalar(col(sc, S_R), col(pow2, M_R), XW, None, ALU.mult))
                link(dve.tensor_scalar(col(sc, S_TMP2), col(pow2, M_BIAS), 2.0, None, ALU.mult))
                link(dve.scalar_tensor_tensor(col(sc, S_TMP2), col(pow2, M_GU), 2.0 ** 10, col(sc, S_TMP2),
                                              ALU.mult, ALU.add))
                g, inv_g = col(sc, S_BASE), col(sc, S_HID)
                link(dve.tensor_scalar(g.bitcast(I32), col(sc, S_TMP2).bitcast(I32), 0x7F800000, None, ALU.bitwise_and))
                link(dve.tensor_scalar(inv_g.bitcast(I32), g.bitcast(I32), -1.0, float(0x7F000000), ALU.mult, ALU.add))
                link(dve.tensor_scalar(inv_g, inv_g, inv_g, 2.0 ** 12, ALU.mult, ALU.mult))
                link(dve.tensor_scalar(g, g, g, 2.0 ** -13 / W_UP, ALU.mult, ALU.mult))
                link(dve.tensor_scalar(g, g, col(pow2, M_DOWN), None, ALU.mult))
                dve.tensor_scalar(inv2[:, M_WO:N_MAG], inv2[:, M_WO:N_MAG], W_UP, None, ALU.mult).then_inc(scales_ready, 1)

            def more_weights():
                dve.wait_ge(scales_ready, 2)
                dve.wait_ge(wo_hi, 1)
                low(w_o[:, 1, :], wo_raw, col(inv2, M_WO), w_o[:, 0, :], wo_split)
                dve.wait_ge(wsh_hi, 3)
                low(w_r[:, 1, :], r_raw, col(inv2, M_R), w_r[:, 0, :], wsh_split)

            def stage_stats(which, src, tile):
                dve.bn_stats(stats[:, which, :], src).then_inc(ln_chain[which], 1)
                dve.wait_ge(ln_chain[which], tile + 1)
                plain(dve)
                dve.bn_aggr(moments[:, which, :], stats[:, which, :]).then_inc(ln_var[which], 1)

            def expert_magnitudes(e, part):
                if part == 0:
                    dve.wait_ge(expert_in, 16 * (e + 1))
                    wait(dve, e_mags_stored, 16 * e)
                    spans = ((0, 0, GU // 2), (1, GU // 2, GU // 2))
                else:
                    spans = ((2, GU, WE - GU),)
                for n, start, size in spans:
                    plain(dve)
                    dve.tensor_reduce(emag[:, n:n + 1], exp_raw[:, bass.ds(e * WE + start, size)], AX.X, ALU.max,
                                      apply_absolute_value=True).then_inc(e_mags, 1)

            def expert_scales(e):
                steps = [0]

                def then(ins):
                    steps[0] += 1
                    ins.then_inc(e_chain, 1)
                    dve.wait_ge(e_chain, 5 * e + steps[0])

                dve.wait_ge(e_mags_back, 16 * (e + 1))
                plain(dve)
                then(dve.tensor_reduce(emax[:, :], mag_rows[:, 0:3 * P].rearrange("p (q n) -> p n q", q=P), AX.X, ALU.max))
                then(dve.tensor_scalar(emax[:, 1:3], emax[:, 1:3], TINY, None, ALU.max))
                then(dve.tensor_tensor(emax[:, 1:2], emax[:, 0:1], emax[:, 1:2], ALU.max))
                p2 = epow[:, bass.ds(e, 1), :].rearrange("p o n -> p (o n)")
                i2 = einv[:, bass.ds(e, 1), :].rearrange("p o n -> p (o n)")
                then(dve.tensor_scalar(p2.bitcast(I32), emax[:, 1:3].bitcast(I32), 0x7F800000, None, ALU.bitwise_and))
                then(dve.tensor_scalar(i2.bitcast(I32), p2.bitcast(I32), -1.0, float(0x7F000000), ALU.mult, ALU.add))
                dve.tensor_scalar(esc[:, bass.ds(e, 1), :].rearrange("p o n -> p (o n)"), i2, W_UP, None, ALU.mult
                                  ).then_inc(e_scales_ready, 1)

            def step(b, j):
                tile = TPB * b + j
                t1, t2, t3, t4 = [tile - n for n in range(1, 5)]
                e = found(b)
                if live(t3):
                    dve.wait_ge(proj_mm, t3 + 1)
                    wait(dve, x1b_ready, t3)
                    wait(dve, xn2_ready, t3)
                    dve.scalar_tensor_tensor(x1, bank(5), col(sc, S_X1), x_in[:, (j + 1) % 4, 0:H], ALU.mult,
                                             ALU.add).then_inc(x1_ready, 1)
                    dve.wait_ge(x1_ready, t3 + 1)
                    stage_stats(1, x1, t3)
                if live(t4):
                    dve.wait_ge(hidT_hi, t4 + 1)
                    dve.wait_ge(logits_ready, 2 * (t4 + 1))
                    low(flat(hidT[:, 1, :, :]), psum[:, 4, 0:I], col(sc, S_HID), flat(hidT[:, 0, :, :]), hidT_ready)
                if live(t2):
                    for n in range(2):
                        dve.wait_ge(probsT_hi, 2 * t2 + n + 1)
                        low(probsT[:, 1, 4 * n:4 * n + 4, :].rearrange("p r q -> p (r q)"), bank(n), P_UP,
                            probsT[:, 0, 4 * n:4 * n + 4, :].rearrange("p r q -> p (r q)"), probsT_ready)
                if live(tile):
                    dve.wait_ge(x_loaded[j], 16 * (b + 1))
                    stage_stats(0, x_in[:, j, 0:H], tile)
                if live(t1):
                    dve.wait_ge(qT_hi, t1 + 1)
                    low(flat(qT[:, 1, :, :]), bank(5), Q_DOWN, flat(qT[:, 0, :, :]), qT_ready)
                if live(t2):
                    dve.wait_ge(av_mm, t2 + 1)
                    av = psum[:, 0:2, 0:4 * 2 * VW].rearrange("p n (q w) -> p n q w", w=VW)
                    dve.reciprocal(recip[:, :].rearrange("p (n q) -> p n q", n=2), av[:, :, :, HD]).then_inc(recip_ready, 1)
                    dve.wait_ge(recip_ready, t2 + 1)
                    wait(dve, attnT_mm, t2)
                    dve.tensor_tensor(attn[:, :, :].rearrange("p (n q) d -> p n q d", n=2), av[:, :, :, 0:HD],
                                      recip[:, :].rearrange("p (n q) -> p n q", n=2)[:, :, :, None].to_broadcast(
                                          [P, 2, NH // 2, HD]), ALU.mult).then_inc(attn_ready, 1)
                if live(t4):
                    dve.wait_ge(down_mm, t4 + 1)
                    dve.wait_ge(x1b_ready, t4 + 1)
                    dve.scalar_tensor_tensor(base, bank(7), col(sc, S_BASE), base, ALU.mult, ALU.add).then_inc(base_ready, 1)
                if live(t3):
                    dve.wait_ge(xn2T_hi, t3 + 1)
                    low(flat(xn2T[:, 1, :, :]), bank(6), X_UP, flat(xn2T[:, 0, :, :]), xn2T_ready)
                if live(t1):
                    dve.wait_ge(scores_mm, t1 + 1)
                    wait(dve, probsT_mm, t1)
                    scores = bank(2, 2).rearrange("p (h k) -> p h k", k=SK)
                    if j == 1:
                        dve.tensor_tensor(probs[:, :, :], scores, mask[:, None, :].to_broadcast([P, NH, SK]),
                                          ALU.min).then_inc(masked, 1)
                        dve.wait_ge(masked, b + 1)
                        scores = probs[:, :, :]
                    dve.tensor_reduce(head_max[:, :], scores, AX.X, ALU.max).then_inc(max_ready, 1)
                if live(t2):
                    dve.wait_ge(attnT_hi, t2 + 1)
                    dve.tensor_tensor(flat(attnT[:, 1, :, :]), bank(4), flat(attnT[:, 0, :, :]),
                                      ALU.subtract).then_inc(attnT_ready, 1)
                if live(t1):
                    dve.wait_ge(max_ready, t1 + 1)
                    dve.tensor_tensor(probs[:, :, :], scores, head_max[:, :, None].to_broadcast([P, NH, SK]),
                                      ALU.subtract).then_inc(shifted, 1)
                if live(t3):
                    dve.wait_ge(gu_mm, t3 + 1)
                    dve.scalar_tensor_tensor(gate_up[:, :], bank(6), col(sc, S_GU), sh_bias[:, :], ALU.mult,
                                             ALU.add).then_inc(gu_ready, 1)
                if live(tile):
                    dve.wait_ge(xn1T_hi, tile + 1)
                    low(flat(xn1T[:, 1, :, :]), bank(7), X_UP, flat(xn1T[:, 0, :, :]), xn1T_ready)
                if live(t3):
                    dve.wait_ge(tanh_ready, t3 + 1)
                    dve.wait_ge(gu_prod, t3 + 1)
                    dve.scalar_tensor_tensor(hid[:, :], hid[:, :], 1.0, gate_up[:, I:2 * I],
                                             ALU.add, ALU.mult).then_inc(hid_ready, 1)
                early = isinstance(b, int) and b == 0
                if e is not None and j in (1 if early else 0, 2):
                    expert_magnitudes(e, j // 2)
                if e is not None and j == 3:
                    expert_scales(e)
                if isinstance(b, int) and (b, j) == (0, 0):
                    first_weights()
                    more_scales()
                if isinstance(b, int) and (b, j) == (0, 1):
                    more_weights()

            dve.wait_ge(const_ready, 2)
            over_tiles(dve, step, 4)

            links[0] = 0

            def link(ins):
                links[0] += 1
                ins.then_inc(route_chain, 1)
                dve.wait_ge(route_chain, links[0])

            def by_te(a):
                return a.rearrange("p (t e) -> p t e", **te)

            def by_et(a):
                return a.rearrange("p (e t) -> p e t", **te)

            def over_e(a):
                return a[:, :, None].to_broadcast([P, T, E])

            dve.wait_ge(logits_ready, 2 * T)
            dve.wait_ge(route_const, 9)
            lg = logits[:, :, :]
            top = small[:, 2 * T:3 * T]
            best = picked[:, 0, 0, :]

            def pick(values, oneh):
                link(dve.tensor_reduce(best, values, AX.X, ALU.max))
                link(dve.tensor_tensor(by_te(eq), values, over_e(best), ALU.is_equal))
                link(dve.tensor_tensor(eq, eq, rev, ALU.mult))
                link(dve.tensor_reduce(top, by_te(eq), AX.X, ALU.max))
                link(dve.tensor_tensor(by_te(oneh), by_te(eq), over_e(top), ALU.is_equal))

            pick(lg, oneh1)
            link(dve.scalar_tensor_tensor(second, oneh1, -BIG, logits[:, :, :].rearrange("p t e -> p (t e)"),
                                          ALU.mult, ALU.add))
            pick(by_te(second), oneh2)
            dve.tensor_tensor(both, oneh1, oneh2, ALU.add).then_inc(both_ready, 1)
            link(dve.memset(ones_te, 1.0))
            link(dve.memset(by_et(ones_te)[:, :, 0:1], 0.0))
            dve.wait_ge(rank_mm, 1)
            rank = psum[:, 0, 0:TE]
            link(dve.tensor_copy(by_et(totals), by_te(psum[:, 0, TE:2 * TE]).rearrange("p t e -> p e t")))
            link(dve.tensor_tensor_scan(cum, ones_te, totals, 0.0, ALU.mult, ALU.add))
            link(dve.tensor_tensor(before, cum, totals, ALU.subtract))
            link(dve.tensor_tensor(by_te(rank_all), by_te(rank), by_et(before).rearrange("p e t -> p t e"), ALU.add))
            n_tiles, t_cum, t_before, ones_e = [small[:, 3 * T + 8 * n:3 * T + 8 * n + E] for n in range(4)]
            link(dve.tensor_tensor(by_et(eq), by_et(cum)[:, :, T - 1:T].to_broadcast([P, E, T]), by_et(steps128), ALU.is_gt))
            link(dve.tensor_reduce(n_tiles, by_et(eq), AX.X, ALU.add))
            link(dve.memset(ones_e, 1.0))
            link(dve.tensor_tensor_scan(t_cum, ones_e, n_tiles, 0.0, ALU.mult, ALU.add))
            link(dve.tensor_tensor(t_before, t_cum, n_tiles, ALU.subtract))
            within, first, lo, hi = [picked[:, n, :, :] for n in (1, 2, 3, 4)]
            for k, oneh in enumerate((oneh1, oneh2)):
                link(dve.tensor_tensor(selected, oneh, rank_all, ALU.mult))
                link(dve.tensor_reduce(within[:, k, :], by_te(selected), AX.X, ALU.add))
                link(dve.tensor_tensor(by_te(selected), by_te(oneh), t_before[:, None, :].to_broadcast([P, T, E]), ALU.mult))
                link(dve.tensor_reduce(first[:, k, :], by_te(selected), AX.X, ALU.add))
            link(dve.tensor_copy(picked_i[:, 0, :, :], within))
            link(dve.tensor_scalar(picked_i[:, 1, :, :], picked_i[:, 0, :, :], P - 1, None, ALU.bitwise_and))
            link(dve.tensor_copy(lo, picked_i[:, 1, :, :]))
            link(dve.tensor_scalar(picked_i[:, 1, :, :], picked_i[:, 0, :, :], 7, None, ALU.arith_shift_right))
            link(dve.tensor_copy(hi, picked_i[:, 1, :, :]))
            def hot_high(t, k, n):
                at_t = bass.ds(t, 1)
                dve.tensor_scalar(hot_hi[:, n, :], iota_s, hi[:, k, at_t], token_no[:, at_t], ALU.is_equal,
                                  ALU.mult).then_inc(hot_hi_ready, 1)
                if k == 0:
                    dve.tensor_scalar(hot_lo[:, n, :], iota_p, lo[:, k, at_t], None, ALU.is_equal).then_inc(hot_lo0_ready, 1)

            link(dve.tensor_tensor(hi, hi, first, ALU.add))
            dve.sem_inc(places_ready, 1)
            for t in range(4):
                for k in range(2):
                    hot_high(t, k, 2 * t + k)
            with dve.Fori(1, T // 4) as quad:
                for i in range(4):
                    for k in range(2):
                        dve.wait_ge(hot_used, 8 * quad + (2 * i + k - 7))
                        hot_high(4 * quad + i, k, 2 * i + k)

            exp_f = small[:, 4 * T:4 * T + SLOTS]

            def over_slots(a):
                return a[:, None, :].to_broadcast([P, SLOTS, E])

            link(dve.tensor_tensor(se_tab, over_slots(t_cum), iota_s[:, :, None].to_broadcast([P, SLOTS, E]), ALU.is_le))
            link(dve.tensor_reduce(exp_f, se_tab, AX.X, ALU.add))
            link(dve.tensor_scalar(exp_f, exp_f, float(E - 1), None, ALU.min))
            dve.tensor_copy(expert_of[:, :], exp_f[0:1, :])
            p_gu, p_d, i_gu = epow[:, :, 0], epow[:, :, 1], einv[:, :, 0]
            link(dve.tensor_scalar(e_scales[:, 0, :], p_gu, XW, None, ALU.mult))
            link(dve.tensor_scalar(e_scales[:, 1, :], i_gu, XW * 2.0 ** -5, None, ALU.mult))
            link(dve.scalar_tensor_tensor(e_scales[:, 2, :], p_gu, 2.0 ** 5 / W_UP, p_gu, ALU.mult, ALU.mult))
            link(dve.tensor_tensor(e_scales[:, 2, :], e_scales[:, 2, :], p_d, ALU.mult))
            one_expert = y_scale_at
            for i in range(2):
                dve.wait_ge(xn2_stored[i], 16 * T // 2)
            link(dve.tensor_tensor(one_expert, over_slots(iota_e), exp_f[:, :, None].to_broadcast([P, SLOTS, E]), ALU.is_equal))
            for n, tab in enumerate((gate_scale_at, up_scale_at)):
                link(dve.tensor_tensor(se_tab, one_expert, over_slots(e_scales[:, n, :]), ALU.mult))
                link(dve.tensor_reduce(tab, se_tab, AX.X, ALU.add))
            link(dve.tensor_tensor(y_scale_at, one_expert, over_slots(e_scales[:, 2, :]), ALU.mult))

            dve.wait_ge(hot_used, 2 * T)
            halves = [psum[:, 1, 0:SLOTS], psum[:, 2, 0:SLOTS]]
            fl = [hid[:, n * SLOTS:(n + 1) * SLOTS] for n in range(3)]
            link(dve.tensor_scalar(fl[0], halves[1], 0.0, TOKENS / 2.0, ALU.is_gt, ALU.mult))
            link(dve.tensor_tensor(fl[0], fl[0], halves[1], ALU.add))
            link(dve.tensor_tensor(fl[0], fl[0], halves[0], ALU.add))
            link(dve.tensor_scalar(fl[1], fl[0], 1.0, 0.0, ALU.subtract, ALU.max))
            link(dve.tensor_copy(gather_at, fl[1]))
            link(dve.tensor_scalar(fl[2], fl[0], 0.0, FAR, ALU.is_equal, ALU.mult))
            link(dve.tensor_tensor(fl[2], fl[2], fl[1], ALU.add))
            dve.tensor_copy(add_at, fl[2]).then_inc(list_ready, 1)

            def estep(q, j):
                t = 4 * q + j
                if elive(t - 3):
                    dve.wait_ge(edown_mm, t - 2)
                    wait(dve, y_added, 16 * (t - 4))
                    dve.tensor_scalar(y[:, (j + 1) % 2, :], bank(3), y_w[:, (j + 1) % 2, :], None, ALU.mult
                                      ).then_inc(y_ready, 1)
                if elive(t - 2):
                    dve.wait_ge(ehidT_hi, t - 1)
                    dve.tensor_tensor(flat(hidT[:, 1, :, :]), psum[:, 2, 0:I], flat(hidT[:, 0, :, :]),
                                      ALU.subtract).then_inc(ehidT_ready, 1)
                if elive(t - 1):
                    wait(dve, y_w_ready, t - 1)
                    dve.scalar_tensor_tensor(y_w_terms[:, :], x_in[:, (j + 3) % 4, H:ROW], 1.0,
                                             y_scale_at[:, bass.ds(t - 1, 1), :].rearrange("p o e -> p (o e)"),
                                             ALU.mult, ALU.mult).then_inc(y_w_made, 1)
                    dve.wait_ge(y_w_made, t)
                    wait(dve, y_ready, t - 2)
                    dve.tensor_reduce(y_w[:, (j + 1) % 2, :], y_w_terms[:, :], AX.X, ALU.add).then_inc(y_w_ready, 1)
                    dve.wait_ge(silu_ready, t)
                    wait(dve, ehidT_mm, t - 1)
                    dve.scalar_tensor_tensor(hid[:, :], psum[:, 1, I:2 * I], up_scale_at[:, bass.ds(t - 1, 1)], silu_g,
                                             ALU.mult, ALU.mult).then_inc(ehid_ready, 1)
                if elive(t):
                    dve.wait_ge(xgT_hi, t + 1)
                    low(flat(xn2T[:, 1, :, :]), bank(0), X_UP, flat(xn2T[:, 0, :, :]), xgT_ready)

            dve.wait_ge(list_ready, 1)
            dve.wait_ge(base_stored, 16 * T)
            over_list(dve, estep, 3)

        @block.tensor
        def _(pe):
            def transposes(dst, src, n, done):
                for c in range(n):
                    last = pe.transpose(dst[:, c * P:(c + 1) * P], src[:, c * P:(c + 1) * P], ident[:, :])
                last.then_inc(done, 1)

            PASSES = ((0, 0), (0, 1), (1, 0))

            def product(dst, lhsT, rhs, n, done=None):
                for c in range(n):
                    for a, z in PASSES:
                        last = pe.matmul(dst, lhsT(a, c), rhs(z, c), start=(c == 0 and a == z == 0),
                                         stop=(c == n - 1 and a == 1))
                if done is not None:
                    last.then_inc(done, 1)

            def chunks(t4):
                return lambda v, c: t4[:, v, c, :]

            def columns(w, width, first=0):
                return lambda v, c: w[:, v, first + c * width:first + (c + 1) * width]

            def spread_magnitudes(a, z):
                n = z - a
                pe.wait_ge(mags_ready, z)
                pe.transpose(psum[0:n, 6, 0:P], mags[:, a:z], ident[:, :]).then_inc(mags_turned, 1)
                pe.wait_ge(diag_ready, 1 if a == 0 else 2)
                pe.matmul(psum[:, 6, P:P + n], ones_rows[0:n, :], mag_diag[0:n, 0 if a == 0 else 1, 0:n],
                          start=True, stop=True).then_inc(mags_spread, 1)

            def values(b):
                pe.matmul(bank((4 + b) % 8), ctx_sb[:, b, :, :].rearrange("p d k -> p (d k)"), wv_sb,
                          start=True, stop=True).then_inc(v_mm, 1)

            def first_products():
                pe.wait_ge(ctx_in, 4 * 16)
                for c in range(C):
                    last = pe.matmul(psum[:, c, :].rearrange("p (b k) -> p b k", b=B), wk_sb[:, c * P:(c + 1) * P],
                                     ctx_sb[:, :, 0, :], start=True, stop=True)
                last.then_inc(k_mm, 1)
                spread_magnitudes(0, M_WO)
                pe.wait_ge(scales_ready, 1)
                pe.wait_ge(xn1T_ready, 1)
                for b in range(4):
                    values(b)
                pe.wait_ge(k_split, 1)
                for b in range(4, B):
                    values(b)
                pe.wait_ge(v_split, 2)

            pe.wait_ge(const_ready, 3)

            def step(b, j):
                tile = TPB * b + j
                t1, t2, t3, t4 = [tile - n for n in range(1, 5)]
                if live(t2):
                    pe.wait_ge(probs_ready, t2 + 1)
                    wait(pe, attn_ready, t2)
                    transposes(bank(0, 2), probs_flat, PAIRS, probsT_mm)
                if live(t1):
                    pe.wait_ge(xn1T_ready, t1 + 1)
                    wait(pe, x1_ready, t3 + 1 if live(t3) else 0)
                    if isinstance(t1, int) and t1 == 0:
                        pe.wait_ge(wq_split, 1)
                    for o in range(C):
                        for c in range(C):
                            for a, z in PASSES:
                                last = pe.matmul(psum[:, 5, o * P:(o + 1) * P],
                                                 w_q[:, a, c * H + o * P:c * H + (o + 1) * P], xn1T[:, z, c, :],
                                                 start=(c == 0 and a == z == 0), stop=(c == C - 1 and a == 1))
                    last.then_inc(q_mm, 1)
                if isinstance(b, int) and (b, j) == (0, 1):
                    spread_magnitudes(M_WO, N_MAG)
                if live(t2):
                    pe.wait_ge(probsT_ready, 2 * (t2 + 1))
                    if j == 2:
                        pe.wait_ge(v_bd_ready, 2 * (b + 1))
                    for r in range(PAIRS):
                        dst = psum[:, r // 4, (r % 4) * 2 * VW:(r % 4 + 1) * 2 * VW]
                        for a, z in PASSES:
                            last = pe.matmul(dst, probsT[:, a, r, :], v_bd[:, z, r, :, :].rearrange("p h w -> p (h w)"),
                                             start=(a == z == 0), stop=(a == 1))
                    last.then_inc(av_mm, 1)
                if live(t4):
                    pe.wait_ge(hidT_ready, t4 + 1)
                    wait(pe, xn1T_ready, t1 + 1 if live(t1) else T)
                    product(bank(7), chunks(hidT), columns(w_sh, H, GU), CI, down_mm)
                if live(t3):
                    pe.wait_ge(xn2_ready, t3 + 1)
                    wait(pe, gu_ready, t3)
                    transposes(bank(6), xn2[:, (j + 1) % 2, :], C, xn2T_mm)
                if live(t1):
                    pe.wait_ge(qT_ready, t1 + 1)
                    if isinstance(t1, int) and t1 == 0:
                        pe.wait_ge(v_split, 4)
                    wait(pe, shifted, t1)
                    if j == 1:
                        pe.wait_ge(k_bd_ready, HPC * (b + 1))
                    for c in range(C):
                        dst = psum[:, 2 + c // 2, (c % 2) * 2 * P:(c % 2) * 2 * P + 2 * P]
                        for a, z in PASSES:
                            last = pe.matmul(dst, qT[:, a, c, :], k_bd[:, z, c, :, :].rearrange("p h k -> p (h k)"),
                                             start=(a == z == 0), stop=(a == 1))
                    last.then_inc(scores_mm, 1)
                if live(t2):
                    pe.wait_ge(attn_ready, t2 + 1)
                    wait(pe, hidT_ready, t4 + 1 if live(t4) else 0)
                    transposes(bank(4), attn_flat, C, attnT_mm)
                if live(t3):
                    pe.wait_ge(xn2T_ready, t3 + 1)
                    if isinstance(t3, int) and t3 == 0:
                        pe.wait_ge(wsh_split, 3)
                    product(bank(6), chunks(xn2T), columns(w_sh, 2 * I), C, gu_mm)
                if live(tile):
                    pe.wait_ge(xn1_ready, tile + 1)
                    wait(pe, base_ready, t4 + 1 if live(t4) else 0)
                    transposes(bank(7), xn1[:, :], C, xn1T_mm)
                if live(t2):
                    pe.wait_ge(attnT_ready, t2 + 1)
                    wait(pe, qT_ready, t1 + 1 if live(t1) else T)
                    if isinstance(t2, int) and t2 == 0:
                        pe.wait_ge(wo_split, 1)
                    product(bank(5), chunks(attnT), columns(w_o, H), C, proj_mm)
                if live(t3):
                    pe.wait_ge(hid_ready, t3 + 1)
                    wait(pe, attnT_ready, t2 + 1 if live(t2) else T)
                    product(psum[:, 4, I:I + E], chunks(xn2T), columns(w_r, E), C)
                    transposes(psum[:, 4, :], hid, CI, hidT_mm)
                if isinstance(b, int) and (b, j) == (0, 0):
                    first_products()

            over_tiles(pe, step, 4)

            pe.wait_ge(both_ready, 1)
            pe.wait_ge(route_const, 3)
            pe.wait_ge(attn_ready, T)
            pe.matmul(psum[:, 0, 0:TE], tri, both, start=True, stop=True)
            pe.matmul(psum[:, 0, TE:2 * TE], ones_pp, both, start=True, stop=True).then_inc(rank_mm, 1)

            def place(t, k, n, half, first, last):
                pe.wait_ge(hot_hi_ready, 2 * t + k + 1)
                pe.wait_ge((hot_lo0_ready, hot_lo1_ready)[k], t + 1)
                pe.matmul(psum[:, 1 + half, 0:SLOTS], hot_lo[:, n, :], hot_hi[:, n, :], start=first,
                          stop=last).then_inc(hot_used, 1)

            pe.wait_ge(places_ready, 1)
            for half in range(2):
                def quad_of(quad, first=False, last=False):
                    for i in range(4):
                        for k in range(2):
                            place(4 * quad + i, k, 2 * i + k, half, first and i + k == 0, last and i + k == 4)

                quads = T // 8
                quad_of(half * quads, first=True)
                with pe.Fori(half * quads + 1, half * quads + quads - 1) as quad:
                    quad_of(quad)
                quad_of(half * quads + quads - 1, last=True)

            def expert_weights(e, width, first=0):
                return lambda v, c: w_exp[:, bass.ds(e, 1), v, first + c * width:first + (c + 1) * width].rearrange(
                    "p o w -> p (o w)")

            def estep(q, j):
                t = 4 * q + j
                if elive(t - 1):
                    e_gu = pe.value_load(expert_of[0:1, bass.ds(t - 1, 1)], min_val=0, max_val=E - 1)
                if elive(t - 2):
                    e_down = pe.value_load(expert_of[0:1, bass.ds(t - 2, 1)], min_val=0, max_val=E - 1)
                    pe.wait_ge(ehid_ready, t - 1)
                    wait(pe, ehidT_ready, t - 2)
                    transposes(bank(2), hid, CI, ehidT_mm)
                if elive(t - 1):
                    pe.wait_ge(xgT_ready, t)
                    product(bank(1), chunks(xn2T), expert_weights(e_gu, 2 * I), C, egu_mm)
                if elive(t):
                    pe.wait_ge(gathered[j], 16 * (q + 1))
                    wait(pe, xgT_ready, t)
                    transposes(bank(0), x_in[:, j, :], C, xg_mm)
                if elive(t - 2):
                    pe.wait_ge(ehidT_ready, t - 1)
                    wait(pe, y_ready, t - 2)
                    product(bank(3), chunks(hidT), expert_weights(e_down, H, GU), CI, edown_mm)

            pe.wait_ge(list_ready, 1)
            pe.wait_ge(piece_split, E * PIECES)
            over_list(pe, estep, 2)


def kernel(**inputs):
    import numpy as np
    import concourse.bacc as bacc
    from concourse.bass_utils import run_bass_kernel_spmd as run

    a = {n: np.asarray(v) for n, v in inputs.items()}

    def rows(w):
        return w.reshape(-1, P, w.shape[-1]).transpose(1, 0, 2)

    def ffn(wg, wu, wd):
        gu = np.concatenate([rows(wg), rows(wu)], axis=2)
        return np.concatenate([gu.reshape(P, -1), rows(wd).reshape(P, -1)], axis=1)

    wg, wu, wd = (a["L0_ffn_" + n] for n in ("wg", "wu", "wd"))
    wkv = a["L0_xattn_Wkv_expand"]
    arrays = {
        "x": a["x"].reshape(TOKENS, H),
        "ctxT": a["ctx_512"].transpose(2, 0, 1),
        "wqT": rows(a["L0_xattn_Wq"].T).reshape(P, -1),
        "wkT": wkv[:H].T,
        "wvT": wkv[H:].T,
        "woT": rows(a["L0_xattn_Wout"].T).reshape(P, -1),
        "routerT": rows(a["L0_ffn_router_w"].T).reshape(P, -1),
        "experts": np.stack([ffn(wg[e], wu[e], wd[e]) for e in range(E)], axis=1),
        "shared": ffn(a["L0_ffn_sg_w"], a["L0_ffn_su_w"], a["L0_ffn_sd_w"]),
        "sh_b": np.concatenate([a["L0_ffn_sg_b"], a["L0_ffn_su_b"]]),
        "sd_b": a["L0_ffn_sd_b"],
    }
    arrays = {n: np.ascontiguousarray(v) for n, v in arrays.items()}
    nc = bacc.Bacc("TRN2", target_bir_lowering=False, num_devices=1)
    args = [nc.dram_tensor(n, v.shape, mybir.dt.from_np(v.dtype), kind="ExternalInput").ap() for n, v in arrays.items()]
    out = nc.dram_tensor("out", [TOKENS, H], F32, kind="ExternalOutput").ap()
    xattn_moe(nc, *args, out)
    r = run(nc, [arrays], core_ids=[0])
    return r.results[0]["out"].reshape(B, S, H)
```

```python
import concourse.bass as bass
from concourse import mybir
from contextlib import ExitStack

F32 = mybir.dt.float32
F16 = mybir.dt.float16
I32 = mybir.dt.int32
U32 = mybir.dt.uint32
ALU = mybir.AluOpType
ACT = mybir.ActivationFunctionType
AX = mybir.AxisListType

P = 128
B, S, H = 8, 512, 512
NH, HD = 16, 32
SK, L = 64, 128
E, I = 8, 256
C = H // P
CI = I // P
PAIRS = NH // 2
HPC = P // HD
TPB = S // P
T = B * S // P
TOKENS = T * P
SLOTS = 2 * T + E - 1
VW = HD + 1
ROW = H + E
EPS = 1e-5
BIG = 3.4e38
FAR = 8192.0
TINY = 2.0 ** -50
SCALE = float(HD) ** -0.5
GU = C * 2 * I
WE = GU + CI * H
PIECE = 512
PIECES = WE // PIECE

W_UP = 2.0 ** 14
X_UP = 2.0 ** 11
P_UP = 2.0 ** 14
KV_UP = 2.0 ** 6
Q_DOWN = 2.0 ** -20
XW = 1.0 / (X_UP * W_UP)

M_CTX, M_WK, M_WV, M_WQ, M_WO, M_GU, M_DOWN, M_BIAS, M_R = range(9)
N_MAG = 9
MAGS = N_MAG - M_WO
(S_K, S_V, S_EXP, S_X1, S_GU, S_HID, S_BASE, S_R, S_TMP, S_TMP2) = range(10)
N_SC = 10


def xattn_moe(nc, x, ctxT, wqT, wkT, wvT, woT, routerT, experts, shared, sh_b, sd_b, out):
    xn_dram = nc.dram_tensor("normed_tokens", [TOKENS, ROW], F32, kind="Internal").ap()
    mag_dram = nc.dram_tensor("magnitudes", [E * P * 3], F32, kind="Internal").ap()
    stack = ExitStack()
    with stack:
        def sb(name, shape, dt=F32):
            return stack.enter_context(nc.sbuf_tensor(name, shape, dt))

        def sem(name):
            return stack.enter_context(nc.semaphore(name))

        exp_all = sb("exp_all", [P, WE // 2 + E * WE])
        exp_raw = exp_all[:, WE // 2:]
        w_exp = exp_all[:, 0:E * WE].bitcast(F16).rearrange("p (e v w) -> p e v w", e=E, v=2)
        stage = exp_all[:, 4 * WE:]
        at = 0
        staged = []
        for n in (B * 2 * SK, 512, 512, C * H, C * H, WE, C * E):
            staged.append(stage[:, at:at + n])
            at += n
        ctx_sb, wk_sb, wv_sb, wq_raw, wo_raw, sh_raw, r_raw = staged
        ctx_sb = ctx_sb.rearrange("p (b d k) -> p b d k", b=B, d=2)
        w_sh = sb("w_sh", [P, 2, WE], F16)
        w_q = sb("w_q", [P, 2, C * H], F16)
        w_o = sb("w_o", [P, 2, C * H], F16)
        w_r = sb("w_r", [P, 2, C * E], F16)
        sizes = (C * B * SK, B * PAIRS * HD, C * HPC * SK, PAIRS * 2 * VW)
        kv_store = sb("kv_store", [P, sum(sizes)])[:, :]
        k_all, v_all, k_bd, v_bd = [kv_store[:, sum(sizes[:n]):sum(sizes[:n + 1])].bitcast(F16) for n in range(4)]
        k_all = k_all.rearrange("p (v c k) -> p v c k", v=2, c=C)
        v_all = v_all.rearrange("p (v b r d) -> p v b r d", v=2, b=B, r=PAIRS)
        k_bd = k_bd.rearrange("p (v c h k) -> p v c h k", v=2, c=C, h=HPC)
        v_bd = v_bd.rearrange("p (v r h w) -> p v r h w", v=2, r=PAIRS, h=2)
        bd_flat = kv_store[:, sum(sizes[:2]):]
        ident = sb("ident", [P, P])
        sh_bias = sb("sh_bias", [P, 2 * I])
        sd_bias = sb("sd_bias", [P, H])
        mask = sb("mask", [P, SK])
        minus_half = sb("minus_half", [P, 1])
        mags = sb("mags", [P, N_MAG])
        maxima = sb("maxima", [P, N_MAG])
        mag_max = sb("mag_max", [MAGS, 2])
        mag_diag = sb("mag_diag", [MAGS, 2, MAGS])
        ones_rows = sb("ones_rows", [MAGS, P])
        pow2 = sb("pow2", [P, N_MAG])
        inv2 = sb("inv2", [P, N_MAG])
        sc = sb("sc", [P, N_SC])
        emag = sb("emag", [P, 3])
        emax = sb("emax", [P, 3])
        epow = sb("epow", [P, E, 2])
        einv = sb("einv", [P, E, 2])
        esc = sb("esc", [P, E, 2])
        x_in = sb("x_in", [P, 4, ROW])
        xn1 = sb("xn1", [P, H])
        xn1T = sb("xn1T", [P, 2, C, P], F16)
        qT = sb("qT", [P, 2, C, P], F16)
        probs = sb("probs", [P, NH, SK])
        probsT = sb("probsT", [P, 2, PAIRS, P], F16)
        attn = sb("attn", [P, NH, HD])
        attnT = sb("attnT", [P, 2, C, P], F16)
        xy = sb("xy", [P, 2, H])
        x1, base = xy[:, 0, :], xy[:, 1, :]
        xn2 = sb("xn2", [P, 2, ROW])
        xn2T = sb("xn2T", [P, 2, C, P], F16)
        gate_up = sb("gate_up", [P, 2 * I])
        hid = sb("hid", [P, I])
        shared_y = sb("shared_y", [P, H])
        hidT = sb("hidT", [P, 2, CI, P], F16)
        piece = sb("piece", [P, PIECE])
        mag_rows = sb("mag_rows", [P, P * 3])
        stats = sb("stats", [P, 2, 6])
        moments = sb("moments", [P, 2, 2])
        rstd = sb("rstd", [P, 2, 3])
        recip = sb("recip", [P, NH])
        head_max = sb("head_max", [P, NH])
        logits = sb("logits", [P, T, E])
        TE = T * E

        def scratch(n):
            return kv_store[:, n * TE:(n + 1) * TE]

        (eq, oneh1, oneh2, second, both, totals, ones_te, cum, before, rank_all, selected,
         steps128, rev) = [scratch(n) for n in range(13)]
        te = dict(t=T, e=E)
        xn2_flat = xn2[:, :, :].rearrange("p a h -> p (a h)")
        tri = xn1[:, 0:P]
        ones_pp = xn1[:, P:2 * P]
        iota_p = xn1[:, 2 * P:3 * P]
        iota_s = xn1[:, 3 * P:3 * P + SLOTS]
        probs_flat = probs[:, :, :].rearrange("p h k -> p (h k)")
        QUADS = T // 4
        hot_lo = probs_flat.bitcast(F16).rearrange("p (n k i q) -> p n k i q", n=2, k=2, i=4)
        hot_at, hot_hi = [a[:, 0:16 * SLOTS].rearrange("p (n k i s) -> p n k i s", n=2, k=2, i=4) for a in (
            kv_store[:, 13 * TE:13 * TE + 8 * SLOTS].bitcast(F16), probsT[:, :, :, :].rearrange("p v r q -> p (v r q)"))]
        rest = kv_store[:, 13 * TE + 8 * SLOTS:]
        small = rest[:, 0:8 * T]
        picked = rest[:, 256:256 + 12 * T].rearrange("p (n k t) -> p n k t", n=6, k=2)
        picked_i = rest[:, 640:640 + 4 * T].bitcast(I32).rearrange("p (n k t) -> p n k t", n=2, k=2)
        SE = SLOTS * E
        se_tab = rest[:, 768:768 + SE].rearrange("p (s e) -> p s e", e=E)
        iota_e = rest[:, 1360:1360 + E]
        e_scales = rest[:, 1368:1368 + 3 * E].rearrange("p (n e) -> p n e", n=3)
        token_no = small[:, 0:T]
        y_scale_at = xn2_flat[:, 0:SE].rearrange("p (s e) -> p s e", e=E)
        at_tabs = [gate_up[:, n * SLOTS:(n + 1) * SLOTS] for n in range(4)]
        gate_scale_at, up_scale_at = at_tabs[0:2]
        gather_at, add_at = [a.bitcast(U32) for a in at_tabs[2:4]]
        expert_of = sb("expert_of", [1, SLOTS], I32)
        gather_now = sb("gather_now", [P, 4], U32)
        add_now = sb("add_now", [P, 2], U32)
        xgT = [xn2T, attnT]
        XG_BANK, GU_BANK, HT_BANK, DOWN_BANK = (0, 4), 1, 2, 3
        y = xy
        attn_flat = attn[:, :, :].rearrange("p h d -> p (h d)")
        silu_g = attn_flat[:, 0:I]
        y_w = sb("y_w", [P, 2, 1])
        y_w_terms = sb("y_w_terms", [P, E])

        psum = stack.enter_context(nc.psum_tensor("psum", [P, 8, 512], F32))

        def bank(n, k=1):
            return psum[:, n:n + k, :].rearrange("p n w -> p (n w)")

        def flat(t4):
            return t4.rearrange("p c q -> p (c q)")

        waits_met = sem("waits_met")
        ctx_in, wq_in, wo_in, wsh_in, bias_in = [sem(n) for n in ("ctx_in", "wq_in", "wo_in", "wsh_in", "bias_in")]
        const_made, const_ready, kv_zeroed = sem("const_made"), sem("const_ready"), sem("kv_zeroed")
        mags_ready, mags_turned, diag_ready, mags_spread, scale_chain, scales_ready = [sem(n) for n in (
            "mags_ready", "mags_turned", "diag_ready", "mags_spread", "scale_chain", "scales_ready")]
        wq_hi, wq_split, wo_hi, wo_split, wsh_hi, wsh_split = [sem(n) for n in (
            "wq_hi", "wq_split", "wo_hi", "wo_split", "wsh_hi", "wsh_split")]
        k_mm, k_hi, k_split, v_mm, v_hi, v_split, k_bd_ready, v_bd_ready = [sem(n) for n in (
            "k_mm", "k_hi", "k_split", "v_mm", "v_hi", "v_split", "k_bd_ready", "v_bd_ready")]
        expert_in, e_mags, e_mags_stored, e_mags_back, e_chain, e_scales_ready, piece_hi, piece_split = [
            sem(n) for n in ("expert_in", "e_mags", "e_mags_stored", "e_mags_back", "e_chain", "e_scales_ready",
                             "piece_hi", "piece_split")]
        x_loaded = [sem(f"x_loaded{i}") for i in range(4)]
        ln_chain = [sem("ln1_chain"), sem("ln2_chain")]
        ln_var = [sem("ln1_var"), sem("ln2_var")]
        ln_eps = [sem("ln1_eps"), sem("ln2_eps")]
        ln_pow = [sem("ln1_pow"), sem("ln2_pow")]
        ln_rstd = [sem("ln1_rstd"), sem("ln2_rstd")]
        xn1_ready, xn1T_mm, xn1T_hi, xn1T_ready, q_mm, qT_hi, qT_ready = [sem(n) for n in (
            "xn1_ready", "xn1T_mm", "xn1T_hi", "xn1T_ready", "q_mm", "qT_hi", "qT_ready")]
        scores_mm, masked, max_ready, shifted, probs_ready = [sem(n) for n in (
            "scores_mm", "masked", "max_ready", "shifted", "probs_ready")]
        probsT_mm, probsT_hi, probsT_ready, av_mm, recip_ready, attn_ready = [sem(n) for n in (
            "probsT_mm", "probsT_hi", "probsT_ready", "av_mm", "recip_ready", "attn_ready")]
        attnT_mm, attnT_hi, attnT_ready, proj_mm, x1_ready, x1b_ready = [sem(n) for n in (
            "attnT_mm", "attnT_hi", "attnT_ready", "proj_mm", "x1_ready", "x1b_ready")]
        xn2_ready, xn2T_mm, xn2T_hi, xn2T_ready, gu_mm, gu_ready, gu_prod, tanh_ready = [sem(n) for n in (
            "xn2_ready", "xn2T_mm", "xn2T_hi", "xn2T_ready", "gu_mm", "gu_ready", "gu_prod", "tanh_ready")]
        hid_ready, hidT_mm, hidT_hi, logits_ready, hidT_ready, down_mm, shared_ready, base_ready, base_stored = [
            sem(n) for n in ("hid_ready", "hidT_mm", "hidT_hi", "logits_ready", "hidT_ready", "down_mm",
                             "shared_ready", "base_ready", "base_stored")]
        xn2_stored = [sem(f"xn2_stored{i}") for i in range(2)]
        route_const, route_chain, both_ready, rank_mm = [sem(n) for n in (
            "route_const", "route_chain", "both_ready", "rank_mm")]
        hot_at_ready, hot_lo_ready, hot_hi_ready, hot_used = [sem(n) for n in (
            "hot_at_ready", "hot_lo_ready", "hot_hi_ready", "hot_used")]
        gather_ready, add_ready, experts_ready, tables_ready = [sem(n) for n in (
            "gather_ready", "add_ready", "experts_ready", "tables_ready")]
        gather_set, add_set = sem("gather_set"), sem("add_set")
        gathered = [sem(f"gathered{i}") for i in range(4)]
        xg_mm, xgT_hi, xgT_ready, egu_mm, silu_ready, ehid_ready, ehidT_mm, ehidT_hi, ehidT_ready = [sem(n) for n in (
            "xg_mm", "xgT_hi", "xgT_ready", "egu_mm", "silu_ready", "ehid_ready", "ehidT_mm", "ehidT_hi",
            "ehidT_ready")]
        edown_mm, y_w_made, y_w_ready, y_ready, y_added = [sem(n) for n in (
            "edown_mm", "y_w_made", "y_w_ready", "y_ready", "y_added")]

        def live(tile):
            return not isinstance(tile, int) or 0 <= tile < T

        def wait(eng, semaphore, value):
            if not isinstance(value, int) or value > 0:
                eng.wait_ge(semaphore, value)

        def plain(eng):
            eng.sem_inc(waits_met, 1)

        def over_tiles(eng, step, behind):
            for b in range(2):
                for j in range(TPB):
                    step(b, j)
            with eng.Fori(2, B) as b:
                for j in range(TPB):
                    step(b, j)
            for j in range(behind):
                step(B + j // TPB, j % TPB)

        def elive(tile):
            return not isinstance(tile, int) or 0 <= tile < SLOTS

        def over_list(eng, step, behind):
            for q in range(2):
                for j in range(4):
                    step(q, j)
            with eng.Fori(2, SLOTS // 4) as q:
                for j in range(4):
                    step(q, j)
            for j in range(SLOTS % 4 + behind):
                step(SLOTS // 4 + j // 4, j % 4)

        def found(e):
            return None if isinstance(e, int) and not 0 <= e < E else e

        def pieces_at(b, j):
            e = found(b - 1)
            return (None, ()) if e is None or j == 0 else (e, (2 * j - 2, 2 * j - 1))

        def raw_piece(e, k):
            return exp_raw[:, bass.ds(e * WE + k * PIECE, PIECE)]

        def split_piece(e, v, k):
            return w_exp[:, bass.ds(e, 1), v, k * PIECE:(k + 1) * PIECE].rearrange("p o w -> p (o w)")

        def value_parts(v, b, h):
            rows = slice(SK * h, SK * h + SK)
            at = (4 + b) % 8
            return v_all[rows, v, b:b + 4, :, :], psum[rows, at:at + 4, :].rearrange(
                "p b (r h d) -> p b r h d", h=2, d=HD)[:, :, :, h, :]

        block = stack.enter_context(nc.Block())

        @block.sync
        def _(sp):
            def load_x(b, j):
                tile = TPB * b + j
                wait(sp, x1_ready, tile - 3)
                sp.dma_start(x_in[:, j, 0:H], x[bass.ds(tile * P, P), :]).then_inc(x_loaded[j], 16)

            def load_expert(e):
                sp.dma_start(exp_raw[:, bass.ds(e * WE, WE)],
                             experts[:, bass.ds(e, 1), :].rearrange("p o w -> p (o w)")).then_inc(expert_in, 16)

            def through_dram(e):
                here = mag_dram[bass.ds(e * P * 3, P * 3)]
                sp.wait_ge(e_mags, 3 * (e + 1))
                sp.dma_start(here.rearrange("(p n) -> p n", n=3), emag[:, :]).then_inc(e_mags_stored, 16)
                sp.wait_ge(e_mags_stored, 16 * (e + 1))
                sp.dma_start(mag_rows[:, :], here.partition_broadcast(P)).then_inc(e_mags_back, 16)

            def step(b, j):
                tile = TPB * b + j
                t4 = tile - 4
                if live(tile + 1) and not (isinstance(b, int) and (b, j) == (0, 0)):
                    load_x(*((b, j + 1) if j < 3 else (b + 1, 0)))
                if live(t4):
                    sp.wait_ge(logits_ready, 2 * (t4 + 1))
                    sp.dma_start(xn_dram[bass.ds(t4 * P, P), :], xn2[:, j % 2, :]).then_inc(xn2_stored[j % 2], 16)
                e = found(b + 1)
                if j == 0 and isinstance(b, int) and b == 2:
                    sp.wait_ge(wsh_split, 3)
                    sp.wait_ge(wo_split, 1)
                    sp.wait_ge(wq_split, 1)
                    sp.wait_ge(k_split, 1)
                    sp.wait_ge(v_split, 4)
                if j == 0 and e is not None:
                    sp.wait_ge(expert_in, 16 * e)
                    load_expert(e)
                if live(t4):
                    sp.wait_ge(base_ready, t4 + 1)
                    sp.dma_start(out[bass.ds(t4 * P, P), :], base).then_inc(base_stored, 16)
                if j == 3 and found(b) is not None:
                    through_dram(b)

            load_x(0, 0)
            sp.dma_start(wk_sb, wkT).then_inc(ctx_in, 16)
            for d in range(2):
                sp.dma_start(ctx_sb[:, :, d, :], ctxT).then_inc(ctx_in, 16)
            sp.dma_start(wv_sb, wvT).then_inc(ctx_in, 16)
            sp.dma_start(wq_raw, wqT).then_inc(wq_in, 16)
            load_x(0, 1)
            sp.dma_start(wo_raw, woT).then_inc(wo_in, 16)
            sp.dma_start(r_raw, routerT).then_inc(wsh_in, 16)
            sp.dma_start(sh_raw, shared).then_inc(wsh_in, 16)
            sp.dma_start(sh_bias[:, :], sh_b.partition_broadcast(P)).then_inc(bias_in, 16)
            sp.dma_start(sd_bias[:, :], sd_b.partition_broadcast(P)).then_inc(bias_in, 16)
            load_expert(0)
            for b in range(3):
                for j in range(TPB):
                    step(b, j)
            with sp.Fori(3, B - 1) as b:
                for j in range(TPB):
                    step(b, j)
            for j in range(TPB):
                step(B - 1, j)
            for j in range(4):
                step(B, j)

        @block.gpsimd
        def _(pool):
            pool.memset(ident[:, :], 0.0).then_inc(const_made, 1)
            pool.memset(mask[:, :], BIG).then_inc(const_made, 1)
            pool.memset(minus_half[:, :], -0.5).then_inc(const_made, 1)
            pool.wait_ge(const_made, 3)
            pool.affine_select(out=ident[:, :], in_=ident[:, :], compare_op=ALU.not_equal, fill=1.0, base=0,
                               pattern=[[-1, P]], channel_multiplier=1).then_inc(const_ready, 1)
            pool.affine_select(out=mask[:, :], in_=mask[:, :], compare_op=ALU.is_ge, fill=-BIG, base=0,
                               pattern=[[-1, SK]], channel_multiplier=1).then_inc(const_ready, 1)
            pool.memset(ones_rows[:, :], 1.0).then_inc(const_ready, 1)
            pool.memset(bd_flat, 0.0).then_inc(kv_zeroed, 1)
            pool.wait_ge(kv_zeroed, 1)
            pool.wait_ge(const_ready, 3)
            for h in range(2):
                pool.memset(v_bd[SK * h:SK * h + SK, 0, :, h, HD:VW], 1.0).then_inc(kv_zeroed, 1)
            pool.wait_ge(kv_zeroed, 3)

            def inv_std(which, tile):
                pool.wait_ge(ln_var[which], tile + 1)
                plain(pool)
                pool.tensor_scalar(rstd[:, which, 0:1], moments[:, which, 1:2], EPS, None, ALU.add).then_inc(ln_eps[which], 1)
                pool.wait_ge(ln_eps[which], tile + 1)
                pool.tensor_tensor(rstd[:, which, 1:2], rstd[:, which, 0:1], minus_half[:, :],
                                   ALU.pow).then_inc(ln_pow[which], 1)
                pool.wait_ge(ln_pow[which], tile + 1)
                plain(pool)
                pool.tensor_scalar(rstd[:, which, 2:3], moments[:, which, 0:1], -1.0, rstd[:, which, 1:2],
                                   ALU.mult, ALU.mult).then_inc(ln_rstd[which], 1)

            def low_piece(e, k):
                pool.wait_ge(piece_hi, 2 * (e * PIECES + k + 1))
                plain(pool)
                pool.tensor_tensor(split_piece(e, 1, k), piece[:, :], split_piece(e, 0, k),
                                   ALU.subtract).then_inc(piece_split, 1)

            def step(b, j):
                tile = TPB * b + j
                t3, t4 = tile - 3, tile - 4
                e, pieces = pieces_at(b, j)
                if live(t3):
                    inv_std(1, t3)
                if live(tile):
                    inv_std(0, tile)
                if pieces:
                    low_piece(e, pieces[0])
                if live(t4):
                    pool.wait_ge(shared_ready, t4 + 1)
                    pool.tensor_tensor(base, base, shared_y[:, :], ALU.add).then_inc(base_ready, 1)
                if live(t3):
                    pool.wait_ge(gu_ready, t3 + 1)
                    pool.tensor_tensor(gate_up[:, I:2 * I], gate_up[:, 0:I], gate_up[:, I:2 * I], ALU.mult).then_inc(gu_prod, 1)
                    wait(pool, base_stored, 16 * t3)
                    if isinstance(t3, int) and t3 == 0:
                        pool.wait_ge(bias_in, 32)
                    pool.tensor_tensor(base, x1, sd_bias[:, :], ALU.add).then_inc(x1b_ready, 1)
                if len(pieces) > 1:
                    low_piece(e, pieces[1])

            over_tiles(pool, step, 4)

            pool.wait_ge(av_mm, T)
            pool.wait_ge(xn1T_mm, T)
            pool.wait_ge(x1_ready, T)
            pool.memset(tri, 1.0).then_inc(route_const, 1)
            pool.memset(ones_pp, 1.0).then_inc(route_const, 1)
            pool.wait_ge(route_const, 1)
            pool.affine_select(out=tri, in_=tri, compare_op=ALU.is_ge, fill=0.0, base=-1,
                               pattern=[[1, P]], channel_multiplier=-1).then_inc(route_const, 1)

            def iota(dst, pattern, base_value, per_partition):
                pool.iota(dst, pattern=pattern, base=base_value, channel_multiplier=per_partition,
                          allow_small_or_imprecise_dtypes=True).then_inc(route_const, 1)

            iota(rev.rearrange("p (t e) -> p t e", **te), [[0, T], [-1, E]], E, 0)
            iota(steps128.rearrange("p (e t) -> p e t", **te), [[0, E], [P, T]], 0, 0)
            iota(iota_p, [[1, P]], 0, 0)
            iota(iota_s, [[1, SLOTS]], 0, 0)
            iota(iota_e, [[1, E]], 0, 0)
            iota(token_no.rearrange("p (h t) -> p h t", h=2), [[0, 2], [P, T // 2]], 1, 1)

            def over_quads(step):
                for n in range(2):
                    step(n, n)
                with pool.Fori(1, QUADS // 2) as two:
                    for n in range(2):
                        step(2 * two + n, n)

            def number(quad, n):
                pool.wait_ge(hot_at_ready, quad + 1)
                if not isinstance(quad, int):
                    pool.wait_ge(hot_used, quad - 1)
                plain(pool)
                pool.tensor_tensor(hot_hi[:, n], hot_at[:, n], token_no[:, None, bass.ds(4 * quad, 4), None].to_broadcast(
                    [P, 2, 4, SLOTS]), ALU.mult).then_inc(hot_hi_ready, 1)

            over_quads(number)

            pool.wait_ge(gather_ready, 1)
            for i in range(2):
                pool.wait_ge(xn2_stored[i], 16 * T // 2)
            pool.wait_ge(base_stored, 16 * T)

            def gather(tile, ring):
                wait(pool, y_w_ready, tile - 3)
                plain(pool)
                pool.tensor_copy(gather_now[:, ring:ring + 1], gather_at[:, bass.ds(tile, 1)]).then_inc(gather_set, 1)
                pool.wait_ge(gather_set, tile + 1)
                plain(pool)
                pool.indirect_dma_start(x_in[:, ring, :], None, xn_dram,
                                        bass.IndirectOffsetOnAxis(gather_now[:, ring:ring + 1], 0)
                                        ).then_inc(gathered[ring], 16)

            def add(tile, ring):
                plain(pool)
                pool.tensor_copy(add_now[:, ring:ring + 1], add_at[:, bass.ds(tile, 1)]).then_inc(add_set, 1)
                pool.wait_ge(add_set, tile + 1)
                pool.wait_ge(y_ready, tile + 1)
                wait(pool, y_added, 16 * tile)
                plain(pool)
                pool.indirect_dma_start(out, bass.IndirectOffsetOnAxis(add_now[:, ring:ring + 1], 0),
                                        y[:, ring, :], None, bounds_check=TOKENS - 1, oob_is_err=False,
                                        compute_op=ALU.add).then_inc(y_added, 16)

            for t in range(8):
                gather(t, t % 4)
                if t == 6:
                    pool.wait_ge(add_ready, 1)
                if t >= 6:
                    add(t - 6, t % 2)
            with pool.Fori(2, SLOTS // 4) as q:
                for j in range(4):
                    gather(4 * q + j, j)
                    add(4 * q + (j - 6), j % 2)
            for t in range(SLOTS // 4 * 4, SLOTS + 6):
                if t < SLOTS:
                    gather(t, t % 4)
                add(t - 6, t % 2)
            pool.wait_ge(y_added, 16 * SLOTS)

        @block.scalar
        def _(act):
            def copy(dst, src, scale, done):
                act.activation(dst, src, ACT.Copy, scale=scale).then_inc(done, 1)

            def first_weights():
                act.wait_ge(scales_ready, 1)
                act.wait_ge(k_mm, 1)
                copy(k_all[:, 0, :, :].rearrange("p c k -> p (c k)"), bank(0, 4), sc[:, S_K:S_K + 1], k_hi)
                copy(w_q[:, 0, :], wq_raw, sc[:, S_TMP:S_TMP + 1], wq_hi)
                for b in (0, 4):
                    act.wait_ge(v_mm, b + 4)
                    for h in range(2):
                        copy(*value_parts(0, b, h), sc[SK * h:SK * h + SK, S_V:S_V + 1], v_hi)

            def more_weights():
                act.wait_ge(wo_in, 16)
                act.wait_ge(wsh_in, 32)
                act.wait_ge(scales_ready, 2)
                copy(w_o[:, 0, :], wo_raw, inv2[:, M_WO:M_WO + 1], wo_hi)
                copy(w_sh[:, 0, 0:GU], sh_raw[:, 0:GU], inv2[:, M_GU:M_GU + 1], wsh_hi)
                copy(w_sh[:, 0, GU:WE], sh_raw[:, GU:WE], inv2[:, M_DOWN:M_DOWN + 1], wsh_hi)
                copy(w_r[:, 0, :], r_raw, inv2[:, M_R:M_R + 1], wsh_hi)

            def batch_keys(b):
                for h in range(HPC):
                    rows = slice(HD * h, HD * h + HD)
                    plain(act)
                    copy(k_bd[rows, :, :, h, :], k_all[rows, :, :, bass.ds(b * SK, SK)], 1.0, k_bd_ready)

            def high_piece(e, k):
                which = 0 if k < GU // PIECE else 1
                esc_now = esc[:, bass.ds(e, 1), which]
                act.wait_ge(e_scales_ready, e + 1)
                wait(act, piece_split, e * PIECES + k)
                plain(act)
                copy(split_piece(e, 0, k), raw_piece(e, k), esc_now, piece_hi)
                copy(piece[:, :], raw_piece(e, k), esc_now, piece_hi)

            def step(b, j):
                tile = TPB * b + j
                t1, t2, t3, t4 = [tile - n for n in range(1, 5)]
                e, pieces = pieces_at(b, j)
                first = isinstance(b, int) and (b, j) == (0, 0)
                if live(t4):
                    act.wait_ge(hidT_mm, t4 + 1)
                    copy(flat(hidT[:, 0, :, :]), psum[:, 4, 0:I], sc[:, S_HID:S_HID + 1], hidT_hi)
                    copy(logits[:, bass.ds(t4, 1), :], psum[:, 4, I:I + E], sc[:, S_R:S_R + 1], logits_ready)
                    copy(xn2[:, j % 2, H:ROW], psum[:, 4, I:I + E], sc[:, S_R:S_R + 1], logits_ready)
                if live(t2):
                    act.wait_ge(probsT_mm, t2 + 1)
                    for n in range(2):
                        copy(probsT[:, 0, 4 * n:4 * n + 4, :], bank(n), P_UP, probsT_hi)
                if live(t3):
                    act.wait_ge(ln_rstd[1], t3 + 1)
                    wait(act, xn2_stored[(j + 1) % 2], 16 * (TPB // 2 * b + (j - 3) // 2))
                    act.activation(xn2[:, (j + 1) % 2, 0:H], x1, ACT.Identity, bias=rstd[:, 1, 2:3],
                                   scale=rstd[:, 1, 1:2]).then_inc(xn2_ready, 1)
                if live(t1):
                    act.wait_ge(q_mm, t1 + 1)
                    copy(flat(qT[:, 0, :, :]), bank(5), Q_DOWN, qT_hi)
                if pieces:
                    high_piece(e, pieces[0])
                if live(t4):
                    act.wait_ge(down_mm, t4 + 1)
                    wait(act, base_ready, t4)
                    copy(shared_y[:, :], bank(7), sc[:, S_BASE:S_BASE + 1], shared_ready)
                if live(t3):
                    act.wait_ge(xn2T_mm, t3 + 1)
                    copy(flat(xn2T[:, 0, :, :]), bank(6), X_UP, xn2T_hi)
                if j == 1 and live(tile):
                    wait(act, av_mm, tile - 1)
                    if isinstance(b, int) and b == 0:
                        act.wait_ge(v_split, 4)
                    for h in range(2):
                        rows = slice(SK * h, SK * h + SK)
                        plain(act)
                        copy(v_bd[rows, :, :, h, 0:HD],
                             v_all[rows, :, bass.ds(b, 1), :, :].rearrange("p v o r d -> p v (o r) d"), 1.0, v_bd_ready)
                if isinstance(b, int) and (b, j) == (0, 2):
                    more_weights()
                if live(tile):
                    act.wait_ge(ln_rstd[0], tile + 1)
                    act.activation(xn1[:, :], x_in[:, j, 0:H], ACT.Identity, bias=rstd[:, 0, 2:3],
                                   scale=rstd[:, 0, 1:2]).then_inc(xn1_ready, 1)
                if live(t2):
                    act.wait_ge(attnT_mm, t2 + 1)
                    copy(flat(attnT[:, 0, :, :]), bank(4), 1.0, attnT_hi)
                if j == 0 and live(tile) and not first:
                    act.wait_ge(scores_mm, tile)
                    batch_keys(b)
                if len(pieces) > 1:
                    high_piece(e, pieces[1])
                if live(tile):
                    act.wait_ge(xn1T_mm, tile + 1)
                    copy(flat(xn1T[:, 0, :, :]), bank(7), X_UP, xn1T_hi)
                if live(t3):
                    act.wait_ge(gu_ready, t3 + 1)
                    act.activation(hid[:, :], gate_up[:, 0:I], ACT.Tanh, scale=0.5).then_inc(tanh_ready, 1)
                if live(t1):
                    act.wait_ge(shifted, t1 + 1)
                    act.activation(probs[:, :, :], probs[:, :, :], ACT.Exp, scale=sc[:, S_EXP:S_EXP + 1]).then_inc(probs_ready, 1)
                if first:
                    first_weights()
                    act.wait_ge(k_split, 1)
                    batch_keys(0)

            over_tiles(act, step, 4)

            def estep(q, j):
                t = 4 * q + j
                if elive(t - 3):
                    act.wait_ge(ehidT_mm, t - 2)
                    copy(flat(hidT[:, 0, :, :]), psum[:, HT_BANK, 0:I], 1.0, ehidT_hi)
                if isinstance(t, int) and t == 2:
                    act.wait_ge(tables_ready, 1)
                if elive(t - 2):
                    act.wait_ge(egu_mm, t - 1)
                    plain(act)
                    act.activation(silu_g, psum[:, GU_BANK, 0:I], ACT.Silu, scale=gate_scale_at[:, bass.ds(t - 2, 1)]
                                   ).then_inc(silu_ready, 1)
                if elive(t):
                    act.wait_ge(xg_mm, t + 1)
                    copy(flat(xgT[j % 2][:, 0, :, :]), bank(XG_BANK[j % 2]), X_UP, xgT_hi)

            act.wait_ge(gather_ready, 1)
            over_list(act, estep, 3)

        @block.vector
        def _(dve):
            links = [0]

            def link(ins):
                links[0] += 1
                ins.then_inc(scale_chain, 1)
                dve.wait_ge(scale_chain, links[0])

            def magnitude(col, src):
                dve.tensor_reduce(mags[:, col:col + 1], src, AX.X, ALU.max, apply_absolute_value=True).then_inc(mags_ready, 1)

            def powers(a, z, group):
                n = z - a
                dve.wait_ge(mags_turned, group)
                link(dve.tensor_reduce(mag_max[0:n, group - 1:group], psum[0:n, 6, 0:P], AX.X, ALU.max))
                dve.tensor_scalar(mag_diag[0:n, group - 1, 0:n], ident[0:n, 0:n], mag_max[0:n, group - 1:group], None,
                                  ALU.mult).then_inc(diag_ready, 1)
                dve.wait_ge(mags_spread, group)
                link(dve.tensor_scalar(maxima[:, a:z], psum[:, 6, P:P + n], TINY, None, ALU.max))
                link(dve.tensor_scalar(pow2[:, a:z].bitcast(I32), maxima[:, a:z].bitcast(I32), 0x7F800000, None,
                                       ALU.bitwise_and))
                link(dve.tensor_scalar(inv2[:, a:z].bitcast(I32), pow2[:, a:z].bitcast(I32), -1.0, float(0x7F000000),
                                       ALU.mult, ALU.add))

            def col(table, n):
                return table[:, n:n + 1]

            def low(dst, src, scale, high, done):
                dve.scalar_tensor_tensor(dst, src, scale, high, ALU.mult, ALU.subtract).then_inc(done, 1)

            def first_weights():
                dve.wait_ge(ctx_in, 64)
                magnitude(M_CTX, staged[0])
                magnitude(M_WK, wk_sb)
                magnitude(M_WV, wv_sb)
                dve.wait_ge(wq_in, 16)
                magnitude(M_WQ, wq_raw)
                powers(0, M_WO, 1)
                link(dve.tensor_scalar(col(sc, S_TMP), col(inv2, M_WQ), W_UP, None, ALU.mult))
                link(dve.tensor_scalar(col(sc, S_K), col(inv2, M_WK), col(inv2, M_CTX), KV_UP, ALU.mult, ALU.mult))
                link(dve.tensor_scalar(col(sc, S_V), col(inv2, M_WV), col(inv2, M_CTX), KV_UP, ALU.mult, ALU.mult))
                link(dve.tensor_scalar(col(sc, S_EXP), col(pow2, M_WK), col(pow2, M_CTX), SCALE * XW / (Q_DOWN * KV_UP),
                                       ALU.mult, ALU.mult))
                dve.tensor_scalar(col(sc, S_EXP), col(sc, S_EXP), col(pow2, M_WQ), None, ALU.mult).then_inc(scales_ready, 1)
                dve.wait_ge(k_hi, 1)
                low(k_all[:, 1, :, :].rearrange("p c k -> p (c k)"), bank(0, 4), col(sc, S_K),
                    k_all[:, 0, :, :].rearrange("p c k -> p (c k)"), k_split)
                for n, b in enumerate((0, 4)):
                    for h in range(2):
                        dve.wait_ge(v_hi, 2 * n + h + 1)
                        dst, src = value_parts(1, b, h)
                        low(dst, src, sc[SK * h:SK * h + SK, S_V:S_V + 1], value_parts(0, b, h)[0], v_split)
                    if n == 0:
                        dve.wait_ge(wq_hi, 1)
                        low(w_q[:, 1, :], wq_raw, col(sc, S_TMP), w_q[:, 0, :], wq_split)

            def more_scales():
                dve.wait_ge(wo_in, 16)
                magnitude(M_WO, wo_raw)
                dve.wait_ge(wsh_in, 32)
                magnitude(M_GU, sh_raw[:, 0:GU])
                magnitude(M_DOWN, sh_raw[:, GU:WE])
                dve.wait_ge(bias_in, 32)
                magnitude(M_BIAS, sh_bias[:, :])
                magnitude(M_R, r_raw)
                powers(M_WO, N_MAG, 2)
                link(dve.tensor_scalar(col(sc, S_X1), col(pow2, M_WV), col(pow2, M_CTX), 1.0 / (KV_UP * W_UP),
                                       ALU.mult, ALU.mult))
                link(dve.tensor_scalar(col(sc, S_X1), col(sc, S_X1), col(pow2, M_WO), None, ALU.mult))
                link(dve.tensor_scalar(col(sc, S_GU), col(pow2, M_GU), XW, None, ALU.mult))
                link(dve.tensor_scalar(col(sc, S_R), col(pow2, M_R), XW, None, ALU.mult))
                link(dve.tensor_scalar(col(sc, S_TMP2), col(pow2, M_BIAS), 2.0, None, ALU.mult))
                link(dve.scalar_tensor_tensor(col(sc, S_TMP2), col(pow2, M_GU), 2.0 ** 10, col(sc, S_TMP2),
                                              ALU.mult, ALU.add))
                g, inv_g = col(sc, S_BASE), col(sc, S_HID)
                link(dve.tensor_scalar(g.bitcast(I32), col(sc, S_TMP2).bitcast(I32), 0x7F800000, None, ALU.bitwise_and))
                link(dve.tensor_scalar(inv_g.bitcast(I32), g.bitcast(I32), -1.0, float(0x7F000000), ALU.mult, ALU.add))
                link(dve.tensor_scalar(inv_g, inv_g, inv_g, 2.0 ** 12, ALU.mult, ALU.mult))
                link(dve.tensor_scalar(g, g, g, 2.0 ** -13 / W_UP, ALU.mult, ALU.mult))
                link(dve.tensor_scalar(g, g, col(pow2, M_DOWN), None, ALU.mult))
                dve.tensor_scalar(inv2[:, M_WO:N_MAG], inv2[:, M_WO:N_MAG], W_UP, None, ALU.mult).then_inc(scales_ready, 1)

            def more_weights():
                dve.wait_ge(scales_ready, 2)
                dve.wait_ge(wo_hi, 1)
                low(w_o[:, 1, :], wo_raw, col(inv2, M_WO), w_o[:, 0, :], wo_split)

            def shared_weights():
                dve.wait_ge(wsh_hi, 3)
                low(w_sh[:, 1, 0:GU], sh_raw[:, 0:GU], col(inv2, M_GU), w_sh[:, 0, 0:GU], wsh_split)
                low(w_sh[:, 1, GU:WE], sh_raw[:, GU:WE], col(inv2, M_DOWN), w_sh[:, 0, GU:WE], wsh_split)
                low(w_r[:, 1, :], r_raw, col(inv2, M_R), w_r[:, 0, :], wsh_split)

            def stage_stats(which, src, tile):
                dve.bn_stats(stats[:, which, :], src).then_inc(ln_chain[which], 1)
                dve.wait_ge(ln_chain[which], tile + 1)
                plain(dve)
                dve.bn_aggr(moments[:, which, :], stats[:, which, :]).then_inc(ln_var[which], 1)

            def expert_magnitudes(e, n):
                if n == 0:
                    dve.wait_ge(expert_in, 16 * (e + 1))
                    wait(dve, e_mags_stored, 16 * e)
                start, size = ((0, GU // 2), (GU // 2, GU // 2), (GU, WE - GU))[n]
                plain(dve)
                dve.tensor_reduce(emag[:, n:n + 1], exp_raw[:, bass.ds(e * WE + start, size)], AX.X, ALU.max,
                                  apply_absolute_value=True).then_inc(e_mags, 1)

            def expert_scales(e):
                steps = [0]

                def then(ins):
                    steps[0] += 1
                    ins.then_inc(e_chain, 1)
                    dve.wait_ge(e_chain, 5 * e + steps[0])

                dve.wait_ge(e_mags_back, 16 * (e + 1))
                plain(dve)
                then(dve.tensor_reduce(emax[:, :], mag_rows[:, 0:3 * P].rearrange("p (q n) -> p n q", q=P), AX.X, ALU.max))
                then(dve.tensor_scalar(emax[:, 1:3], emax[:, 1:3], TINY, None, ALU.max))
                then(dve.tensor_tensor(emax[:, 1:2], emax[:, 0:1], emax[:, 1:2], ALU.max))
                p2 = epow[:, bass.ds(e, 1), :].rearrange("p o n -> p (o n)")
                i2 = einv[:, bass.ds(e, 1), :].rearrange("p o n -> p (o n)")
                then(dve.tensor_scalar(p2.bitcast(I32), emax[:, 1:3].bitcast(I32), 0x7F800000, None, ALU.bitwise_and))
                then(dve.tensor_scalar(i2.bitcast(I32), p2.bitcast(I32), -1.0, float(0x7F000000), ALU.mult, ALU.add))
                dve.tensor_scalar(esc[:, bass.ds(e, 1), :].rearrange("p o n -> p (o n)"), i2, W_UP, None, ALU.mult
                                  ).then_inc(e_scales_ready, 1)

            def step(b, j):
                tile = TPB * b + j
                t1, t2, t3, t4 = [tile - n for n in range(1, 5)]
                e = found(b)
                if live(t3):
                    dve.wait_ge(proj_mm, t3 + 1)
                    wait(dve, x1b_ready, t3)
                    wait(dve, xn2_ready, t3)
                    dve.scalar_tensor_tensor(x1, bank(5), col(sc, S_X1), x_in[:, (j + 1) % 4, 0:H], ALU.mult,
                                             ALU.add).then_inc(x1_ready, 1)
                    dve.wait_ge(x1_ready, t3 + 1)
                    stage_stats(1, x1, t3)
                if live(t4):
                    dve.wait_ge(hidT_hi, t4 + 1)
                    dve.wait_ge(logits_ready, 2 * (t4 + 1))
                    low(flat(hidT[:, 1, :, :]), psum[:, 4, 0:I], col(sc, S_HID), flat(hidT[:, 0, :, :]), hidT_ready)
                if live(t2):
                    for n in range(2):
                        dve.wait_ge(probsT_hi, 2 * t2 + n + 1)
                        low(probsT[:, 1, 4 * n:4 * n + 4, :].rearrange("p r q -> p (r q)"), bank(n), P_UP,
                            probsT[:, 0, 4 * n:4 * n + 4, :].rearrange("p r q -> p (r q)"), probsT_ready)
                if live(tile):
                    dve.wait_ge(x_loaded[j], 16 * (b + 1))
                    stage_stats(0, x_in[:, j, 0:H], tile)
                if live(t1):
                    dve.wait_ge(qT_hi, t1 + 1)
                    low(flat(qT[:, 1, :, :]), bank(5), Q_DOWN, flat(qT[:, 0, :, :]), qT_ready)
                if live(t2):
                    dve.wait_ge(av_mm, t2 + 1)
                    av = psum[:, 0:2, 0:4 * 2 * VW].rearrange("p n (q w) -> p n q w", w=VW)
                    dve.reciprocal(recip[:, :].rearrange("p (n q) -> p n q", n=2), av[:, :, :, HD]).then_inc(recip_ready, 1)
                    dve.wait_ge(recip_ready, t2 + 1)
                    wait(dve, attnT_mm, t2)
                    dve.tensor_tensor(attn[:, :, :].rearrange("p (n q) d -> p n q d", n=2), av[:, :, :, 0:HD],
                                      recip[:, :].rearrange("p (n q) -> p n q", n=2)[:, :, :, None].to_broadcast(
                                          [P, 2, NH // 2, HD]), ALU.mult).then_inc(attn_ready, 1)
                if e is not None and j in ((1, 2, 3) if isinstance(b, int) and b == 0 else (0, 2, 3)):
                    expert_magnitudes(e, max(0, j - 1))
                if isinstance(b, int) and (b, j) == (0, 2):
                    more_weights()
                if live(t3):
                    dve.wait_ge(xn2T_hi, t3 + 1)
                    low(flat(xn2T[:, 1, :, :]), bank(6), X_UP, flat(xn2T[:, 0, :, :]), xn2T_ready)
                if live(t1):
                    dve.wait_ge(scores_mm, t1 + 1)
                    wait(dve, probsT_mm, t1)
                    scores = bank(2, 2).rearrange("p (h k) -> p h k", k=SK)
                    if j == 1:
                        dve.tensor_tensor(probs[:, :, :], scores, mask[:, None, :].to_broadcast([P, NH, SK]),
                                          ALU.min).then_inc(masked, 1)
                        dve.wait_ge(masked, b + 1)
                        scores = probs[:, :, :]
                    dve.tensor_reduce(head_max[:, :], scores, AX.X, ALU.max).then_inc(max_ready, 1)
                if live(t2):
                    dve.wait_ge(attnT_hi, t2 + 1)
                    dve.tensor_tensor(flat(attnT[:, 1, :, :]), bank(4), flat(attnT[:, 0, :, :]),
                                      ALU.subtract).then_inc(attnT_ready, 1)
                if live(t1):
                    dve.wait_ge(max_ready, t1 + 1)
                    dve.tensor_tensor(probs[:, :, :], scores, head_max[:, :, None].to_broadcast([P, NH, SK]),
                                      ALU.subtract).then_inc(shifted, 1)
                if live(t3):
                    dve.wait_ge(gu_mm, t3 + 1)
                    dve.scalar_tensor_tensor(gate_up[:, :], bank(6), col(sc, S_GU), sh_bias[:, :], ALU.mult,
                                             ALU.add).then_inc(gu_ready, 1)
                if live(tile):
                    dve.wait_ge(xn1T_hi, tile + 1)
                    low(flat(xn1T[:, 1, :, :]), bank(7), X_UP, flat(xn1T[:, 0, :, :]), xn1T_ready)
                if live(t3):
                    dve.wait_ge(tanh_ready, t3 + 1)
                    dve.wait_ge(gu_prod, t3 + 1)
                    dve.scalar_tensor_tensor(hid[:, :], hid[:, :], 1.0, gate_up[:, I:2 * I],
                                             ALU.add, ALU.mult).then_inc(hid_ready, 1)
                if j == 0 and found(b - 1) is not None:
                    expert_scales(b - 1)
                if isinstance(b, int) and (b, j) == (0, 0):
                    first_weights()
                if isinstance(b, int) and (b, j) == (0, 1):
                    more_scales()
                if isinstance(b, int) and (b, j) == (0, 2):
                    shared_weights()

            dve.wait_ge(const_ready, 2)
            over_tiles(dve, step, 4)

            links[0] = 0

            def link(ins):
                links[0] += 1
                ins.then_inc(route_chain, 1)
                dve.wait_ge(route_chain, links[0])

            def by_te(a):
                return a.rearrange("p (t e) -> p t e", **te)

            def by_et(a):
                return a.rearrange("p (e t) -> p e t", **te)

            def over_e(a):
                return a[:, :, None].to_broadcast([P, T, E])

            dve.wait_ge(logits_ready, 2 * T)
            dve.wait_ge(route_const, 9)
            lg = logits[:, :, :]
            top = small[:, 2 * T:3 * T]
            best = picked[:, 0, 0, :]

            def pick(values, oneh):
                link(dve.tensor_reduce(best, values, AX.X, ALU.max))
                link(dve.tensor_tensor(by_te(eq), values, over_e(best), ALU.is_equal))
                link(dve.tensor_tensor(eq, eq, rev, ALU.mult))
                link(dve.tensor_reduce(top, by_te(eq), AX.X, ALU.max))
                link(dve.tensor_tensor(by_te(oneh), by_te(eq), over_e(top), ALU.is_equal))

            pick(lg, oneh1)
            link(dve.scalar_tensor_tensor(second, oneh1, -BIG, logits[:, :, :].rearrange("p t e -> p (t e)"),
                                          ALU.mult, ALU.add))
            pick(by_te(second), oneh2)
            dve.tensor_tensor(both, oneh1, oneh2, ALU.add).then_inc(both_ready, 1)
            link(dve.memset(ones_te, 1.0))
            link(dve.memset(by_et(ones_te)[:, :, 0:1], 0.0))
            dve.wait_ge(rank_mm, 1)
            rank = psum[:, 0, 0:TE]
            link(dve.tensor_copy(by_et(totals), by_te(psum[:, 0, TE:2 * TE]).rearrange("p t e -> p e t")))
            link(dve.tensor_tensor_scan(cum, ones_te, totals, 0.0, ALU.mult, ALU.add))
            link(dve.tensor_tensor(before, cum, totals, ALU.subtract))
            link(dve.tensor_tensor(by_te(rank_all), by_te(rank), by_et(before).rearrange("p e t -> p t e"), ALU.add))
            n_tiles, t_cum, t_before, ones_e = [small[:, 3 * T + 8 * n:3 * T + 8 * n + E] for n in range(4)]
            link(dve.tensor_tensor(by_et(eq), by_et(cum)[:, :, T - 1:T].to_broadcast([P, E, T]), by_et(steps128), ALU.is_gt))
            link(dve.tensor_reduce(n_tiles, by_et(eq), AX.X, ALU.add))
            link(dve.memset(ones_e, 1.0))
            link(dve.tensor_tensor_scan(t_cum, ones_e, n_tiles, 0.0, ALU.mult, ALU.add))
            link(dve.tensor_tensor(t_before, t_cum, n_tiles, ALU.subtract))
            within, first, lo, hi = [picked[:, n, :, :] for n in (1, 2, 3, 4)]
            for k, oneh in enumerate((oneh1, oneh2)):
                link(dve.tensor_tensor(selected, oneh, rank_all, ALU.mult))
                link(dve.tensor_reduce(within[:, k, :], by_te(selected), AX.X, ALU.add))
                link(dve.tensor_tensor(by_te(selected), by_te(oneh), t_before[:, None, :].to_broadcast([P, T, E]), ALU.mult))
                link(dve.tensor_reduce(first[:, k, :], by_te(selected), AX.X, ALU.add))
            link(dve.tensor_copy(picked_i[:, 0, :, :], within))
            link(dve.tensor_scalar(picked_i[:, 1, :, :], picked_i[:, 0, :, :], P - 1, None, ALU.bitwise_and))
            link(dve.tensor_copy(lo, picked_i[:, 1, :, :]))
            link(dve.tensor_scalar(picked_i[:, 1, :, :], picked_i[:, 0, :, :], 7, None, ALU.arith_shift_right))
            link(dve.tensor_copy(hi, picked_i[:, 1, :, :]))
            link(dve.tensor_tensor(hi, hi, first, ALU.add))

            def hot(quad, n):
                at_t = bass.ds(4 * quad, 4)
                if not isinstance(quad, int):
                    dve.wait_ge(hot_hi_ready, quad - 1)
                    dve.wait_ge(hot_used, quad - 1)
                plain(dve)
                for dst, nos, place, size, done in ((hot_at, iota_s, hi, SLOTS, hot_at_ready), (hot_lo, iota_p, lo, P, hot_lo_ready)):
                    dve.tensor_tensor(dst[:, n], nos[:, None, None, :].to_broadcast([P, 2, 4, size]),
                                      place[:, :, at_t, None].to_broadcast([P, 2, 4, size]), ALU.is_equal).then_inc(done, 1)

            for n in range(2):
                hot(n, n)
            with dve.Fori(1, QUADS // 2) as two:
                for n in range(2):
                    hot(2 * two + n, n)

            dve.wait_ge(hot_used, QUADS)
            halves = [psum[:, 1, 0:SLOTS], psum[:, 2, 0:SLOTS]]
            fl = [hid[:, n * SLOTS:(n + 1) * SLOTS] for n in range(3)]
            link(dve.tensor_scalar(fl[0], halves[1], 0.0, TOKENS / 2.0, ALU.is_gt, ALU.mult))
            link(dve.tensor_tensor(fl[0], fl[0], halves[1], ALU.add))
            link(dve.tensor_tensor(fl[0], fl[0], halves[0], ALU.add))
            link(dve.tensor_scalar(fl[1], fl[0], 1.0, 0.0, ALU.subtract, ALU.max))
            dve.tensor_copy(gather_at, fl[1]).then_inc(gather_ready, 1)
            link(dve.tensor_scalar(fl[2], fl[0], 0.0, FAR, ALU.is_equal, ALU.mult))
            link(dve.tensor_tensor(fl[2], fl[2], fl[1], ALU.add))
            dve.tensor_copy(add_at, fl[2]).then_inc(add_ready, 1)
            exp_f = small[:, 4 * T:4 * T + SLOTS]

            def over_slots(a):
                return a[:, None, :].to_broadcast([P, SLOTS, E])

            link(dve.tensor_tensor(se_tab, over_slots(t_cum), iota_s[:, :, None].to_broadcast([P, SLOTS, E]), ALU.is_le))
            link(dve.tensor_reduce(exp_f, se_tab, AX.X, ALU.add))
            link(dve.tensor_scalar(exp_f, exp_f, float(E - 1), None, ALU.min))
            dve.tensor_copy(expert_of[:, :], exp_f[0:1, :]).then_inc(experts_ready, 1)
            p_gu, p_d, i_gu = epow[:, :, 0], epow[:, :, 1], einv[:, :, 0]
            link(dve.tensor_scalar(e_scales[:, 0, :], p_gu, XW, None, ALU.mult))
            link(dve.tensor_scalar(e_scales[:, 1, :], i_gu, XW * 2.0 ** -5, None, ALU.mult))
            link(dve.scalar_tensor_tensor(e_scales[:, 2, :], p_gu, 2.0 ** 5 / W_UP, p_gu, ALU.mult, ALU.mult))
            link(dve.tensor_tensor(e_scales[:, 2, :], e_scales[:, 2, :], p_d, ALU.mult))
            one_expert = y_scale_at
            for i in range(2):
                dve.wait_ge(xn2_stored[i], 16 * T // 2)
            link(dve.tensor_tensor(one_expert, over_slots(iota_e), exp_f[:, :, None].to_broadcast([P, SLOTS, E]), ALU.is_equal))
            for n, tab in enumerate((gate_scale_at, up_scale_at)):
                link(dve.tensor_tensor(se_tab, one_expert, over_slots(e_scales[:, n, :]), ALU.mult))
                link(dve.tensor_reduce(tab, se_tab, AX.X, ALU.add))
            dve.tensor_tensor(y_scale_at, one_expert, over_slots(e_scales[:, 2, :]), ALU.mult).then_inc(tables_ready, 1)

            def estep(q, j):
                t = 4 * q + j
                if elive(t - 4):
                    dve.wait_ge(edown_mm, t - 3)
                    wait(dve, y_added, 16 * (t - 5))
                    dve.tensor_scalar(y[:, j % 2, :], bank(DOWN_BANK), y_w[:, j % 2, :], None, ALU.mult
                                      ).then_inc(y_ready, 1)
                if elive(t - 3):
                    dve.wait_ge(ehidT_hi, t - 2)
                    dve.tensor_tensor(flat(hidT[:, 1, :, :]), psum[:, HT_BANK, 0:I], flat(hidT[:, 0, :, :]),
                                      ALU.subtract).then_inc(ehidT_ready, 1)
                if elive(t - 2):
                    wait(dve, y_w_ready, t - 2)
                    dve.scalar_tensor_tensor(y_w_terms[:, :], x_in[:, (j + 2) % 4, H:ROW], 1.0,
                                             y_scale_at[:, bass.ds(t - 2, 1), :].rearrange("p o e -> p (o e)"),
                                             ALU.mult, ALU.mult).then_inc(y_w_made, 1)
                    dve.wait_ge(y_w_made, t - 1)
                    wait(dve, y_ready, t - 3)
                    dve.tensor_reduce(y_w[:, j % 2, :], y_w_terms[:, :], AX.X, ALU.add).then_inc(y_w_ready, 1)
                    dve.wait_ge(silu_ready, t - 1)
                    wait(dve, ehidT_mm, t - 2)
                    dve.scalar_tensor_tensor(hid[:, :], psum[:, GU_BANK, I:2 * I], up_scale_at[:, bass.ds(t - 2, 1)],
                                             silu_g, ALU.mult, ALU.mult).then_inc(ehid_ready, 1)
                if elive(t):
                    dve.wait_ge(xgT_hi, t + 1)
                    low(flat(xgT[j % 2][:, 1, :, :]), bank(XG_BANK[j % 2]), X_UP, flat(xgT[j % 2][:, 0, :, :]), xgT_ready)

            dve.wait_ge(tables_ready, 1)
            dve.wait_ge(base_stored, 16 * T)
            over_list(dve, estep, 4)

        @block.tensor
        def _(pe):
            def transposes(dst, src, n, done):
                for c in range(n):
                    last = pe.transpose(dst[:, c * P:(c + 1) * P], src[:, c * P:(c + 1) * P], ident[:, :])
                last.then_inc(done, 1)

            PASSES = ((0, 0), (0, 1), (1, 0))

            def product(dst, lhsT, rhs, n, done=None):
                for c in range(n):
                    for a, z in PASSES:
                        last = pe.matmul(dst, lhsT(a, c), rhs(z, c), start=(c == 0 and a == z == 0),
                                         stop=(c == n - 1 and a == 1))
                if done is not None:
                    last.then_inc(done, 1)

            def chunks(t4):
                return lambda v, c: t4[:, v, c, :]

            def columns(w, width, first=0):
                return lambda v, c: w[:, v, first + c * width:first + (c + 1) * width]

            def spread_magnitudes(a, z):
                n = z - a
                pe.wait_ge(mags_ready, z)
                pe.transpose(psum[0:n, 6, 0:P], mags[:, a:z], ident[:, :]).then_inc(mags_turned, 1)
                pe.wait_ge(diag_ready, 1 if a == 0 else 2)
                pe.matmul(psum[:, 6, P:P + n], ones_rows[0:n, :], mag_diag[0:n, 0 if a == 0 else 1, 0:n],
                          start=True, stop=True).then_inc(mags_spread, 1)

            def values(b):
                pe.matmul(bank((4 + b) % 8), ctx_sb[:, b, :, :].rearrange("p d k -> p (d k)"), wv_sb,
                          start=True, stop=True).then_inc(v_mm, 1)

            def first_products():
                pe.wait_ge(ctx_in, 4 * 16)
                for c in range(C):
                    last = pe.matmul(psum[:, c, :].rearrange("p (b k) -> p b k", b=B), wk_sb[:, c * P:(c + 1) * P],
                                     ctx_sb[:, :, 0, :], start=True, stop=True)
                last.then_inc(k_mm, 1)
                spread_magnitudes(0, M_WO)
                pe.wait_ge(scales_ready, 1)
                pe.wait_ge(xn1T_ready, 1)
                for b in range(4):
                    values(b)
                pe.wait_ge(k_split, 1)
                for b in range(4, B):
                    values(b)
                pe.wait_ge(v_split, 2)

            pe.wait_ge(const_ready, 3)

            def step(b, j):
                tile = TPB * b + j
                t1, t2, t3, t4 = [tile - n for n in range(1, 5)]
                if live(t2):
                    pe.wait_ge(probs_ready, t2 + 1)
                    wait(pe, attn_ready, t2)
                    transposes(bank(0, 2), probs_flat, PAIRS, probsT_mm)
                if live(t1):
                    pe.wait_ge(xn1T_ready, t1 + 1)
                    wait(pe, x1_ready, t3 + 1 if live(t3) else 0)
                    if isinstance(t1, int) and t1 == 0:
                        pe.wait_ge(wq_split, 1)
                    for o in range(C):
                        for c in range(C):
                            for a, z in PASSES:
                                last = pe.matmul(psum[:, 5, o * P:(o + 1) * P],
                                                 w_q[:, a, c * H + o * P:c * H + (o + 1) * P], xn1T[:, z, c, :],
                                                 start=(c == 0 and a == z == 0), stop=(c == C - 1 and a == 1))
                    last.then_inc(q_mm, 1)
                if isinstance(b, int) and (b, j) == (0, 2):
                    spread_magnitudes(M_WO, N_MAG)
                if live(t2):
                    pe.wait_ge(probsT_ready, 2 * (t2 + 1))
                    if j == 2:
                        pe.wait_ge(v_bd_ready, 2 * (b + 1))
                    for r in range(PAIRS):
                        dst = psum[:, r // 4, (r % 4) * 2 * VW:(r % 4 + 1) * 2 * VW]
                        for a, z in PASSES:
                            last = pe.matmul(dst, probsT[:, a, r, :], v_bd[:, z, r, :, :].rearrange("p h w -> p (h w)"),
                                             start=(a == z == 0), stop=(a == 1))
                    last.then_inc(av_mm, 1)
                if live(t4):
                    pe.wait_ge(hidT_ready, t4 + 1)
                    wait(pe, xn1T_ready, t1 + 1 if live(t1) else T)
                    product(bank(7), chunks(hidT), columns(w_sh, H, GU), CI, down_mm)
                if live(t3):
                    pe.wait_ge(xn2_ready, t3 + 1)
                    wait(pe, gu_ready, t3)
                    transposes(bank(6), xn2[:, (j + 1) % 2, :], C, xn2T_mm)
                if live(t1):
                    pe.wait_ge(qT_ready, t1 + 1)
                    if isinstance(t1, int) and t1 == 0:
                        pe.wait_ge(v_split, 4)
                    wait(pe, shifted, t1)
                    if j == 1:
                        pe.wait_ge(k_bd_ready, HPC * (b + 1))
                    for c in range(C):
                        dst = psum[:, 2 + c // 2, (c % 2) * 2 * P:(c % 2) * 2 * P + 2 * P]
                        for a, z in PASSES:
                            last = pe.matmul(dst, qT[:, a, c, :], k_bd[:, z, c, :, :].rearrange("p h k -> p (h k)"),
                                             start=(a == z == 0), stop=(a == 1))
                    last.then_inc(scores_mm, 1)
                if live(t2):
                    pe.wait_ge(attn_ready, t2 + 1)
                    wait(pe, hidT_ready, t4 + 1 if live(t4) else 0)
                    transposes(bank(4), attn_flat, C, attnT_mm)
                if live(t3):
                    pe.wait_ge(xn2T_ready, t3 + 1)
                    if isinstance(t3, int) and t3 == 0:
                        pe.wait_ge(wsh_split, 3)
                    product(bank(6), chunks(xn2T), columns(w_sh, 2 * I), C, gu_mm)
                if live(tile):
                    pe.wait_ge(xn1_ready, tile + 1)
                    wait(pe, shared_ready, t4 + 1 if live(t4) else 0)
                    transposes(bank(7), xn1[:, :], C, xn1T_mm)
                if live(t2):
                    pe.wait_ge(attnT_ready, t2 + 1)
                    wait(pe, qT_ready, t1 + 1 if live(t1) else T)
                    if isinstance(t2, int) and t2 == 0:
                        pe.wait_ge(wo_split, 1)
                    product(bank(5), chunks(attnT), columns(w_o, H), C, proj_mm)
                if live(t3):
                    pe.wait_ge(hid_ready, t3 + 1)
                    wait(pe, attnT_ready, t2 + 1 if live(t2) else T)
                    product(psum[:, 4, I:I + E], chunks(xn2T), columns(w_r, E), C)
                    transposes(psum[:, 4, :], hid, CI, hidT_mm)
                if isinstance(b, int) and (b, j) == (0, 0):
                    first_products()

            over_tiles(pe, step, 4)

            pe.wait_ge(both_ready, 1)
            pe.wait_ge(route_const, 3)
            pe.wait_ge(attn_ready, T)
            pe.matmul(psum[:, 0, 0:TE], tri, both, start=True, stop=True)
            pe.matmul(psum[:, 0, TE:2 * TE], ones_pp, both, start=True, stop=True).then_inc(rank_mm, 1)

            for quad in range(QUADS):
                half, n = quad // (QUADS // 2), quad % 2
                pe.wait_ge(hot_lo_ready, quad + 1)
                pe.wait_ge(hot_hi_ready, quad + 1)
                for k in range(2):
                    for i in range(4):
                        last = pe.matmul(psum[:, 1 + half, 0:SLOTS], hot_lo[:, n, k, i, :], hot_hi[:, n, k, i, :],
                                         start=(quad % (QUADS // 2) == k == i == 0),
                                         stop=(quad % (QUADS // 2) == QUADS // 2 - 1 and (k, i) == (1, 3)))
                last.then_inc(hot_used, 1)

            def expert_weights(e, width, first=0):
                return lambda v, c: w_exp[:, bass.ds(e, 1), v, first + c * width:first + (c + 1) * width].rearrange(
                    "p o w -> p (o w)")

            def estep(q, j):
                t = 4 * q + j
                if isinstance(t, int) and t == 2:
                    pe.wait_ge(experts_ready, 1)
                if elive(t - 2):
                    e_gu = pe.value_load(expert_of[0:1, bass.ds(t - 2, 1)], min_val=0, max_val=E - 1)
                if elive(t - 3):
                    e_down = pe.value_load(expert_of[0:1, bass.ds(t - 3, 1)], min_val=0, max_val=E - 1)
                    pe.wait_ge(ehid_ready, t - 2)
                    wait(pe, ehidT_ready, t - 3)
                    transposes(bank(HT_BANK), hid, CI, ehidT_mm)
                if elive(t - 2):
                    pe.wait_ge(xgT_ready, t - 1)
                    product(bank(GU_BANK), chunks(xgT[j % 2]), expert_weights(e_gu, 2 * I), C, egu_mm)
                if elive(t):
                    pe.wait_ge(gathered[j], 16 * (q + 1))
                    wait(pe, xgT_ready, t - 1)
                    transposes(bank(XG_BANK[j % 2]), x_in[:, j, :], C, xg_mm)
                if elive(t - 3):
                    pe.wait_ge(ehidT_ready, t - 2)
                    wait(pe, y_ready, t - 3)
                    product(bank(DOWN_BANK), chunks(hidT), expert_weights(e_down, H, GU), CI, edown_mm)

            pe.wait_ge(gather_ready, 1)
            pe.wait_ge(piece_split, E * PIECES)
            over_list(pe, estep, 3)


def kernel(**inputs):
    import numpy as np
    import concourse.bacc as bacc
    from concourse.bass_utils import run_bass_kernel_spmd as run

    a = {n: np.asarray(v) for n, v in inputs.items()}

    def rows(w):
        return w.reshape(-1, P, w.shape[-1]).transpose(1, 0, 2)

    def ffn(wg, wu, wd):
        gu = np.concatenate([rows(wg), rows(wu)], axis=2)
        return np.concatenate([gu.reshape(P, -1), rows(wd).reshape(P, -1)], axis=1)

    wg, wu, wd = (a["L0_ffn_" + n] for n in ("wg", "wu", "wd"))
    wkv = a["L0_xattn_Wkv_expand"]
    arrays = {
        "x": a["x"].reshape(TOKENS, H),
        "ctxT": a["ctx_512"].transpose(2, 0, 1),
        "wqT": rows(a["L0_xattn_Wq"].T).reshape(P, -1),
        "wkT": wkv[:H].T,
        "wvT": wkv[H:].T,
        "woT": rows(a["L0_xattn_Wout"].T).reshape(P, -1),
        "routerT": rows(a["L0_ffn_router_w"].T).reshape(P, -1),
        "experts": np.stack([ffn(wg[e], wu[e], wd[e]) for e in range(E)], axis=1),
        "shared": ffn(a["L0_ffn_sg_w"], a["L0_ffn_su_w"], a["L0_ffn_sd_w"]),
        "sh_b": np.concatenate([a["L0_ffn_sg_b"], a["L0_ffn_su_b"]]),
        "sd_b": a["L0_ffn_sd_b"],
    }
    arrays = {n: np.ascontiguousarray(v) for n, v in arrays.items()}
    nc = bacc.Bacc("TRN2", target_bir_lowering=False, num_devices=1)
    args = [nc.dram_tensor(n, v.shape, mybir.dt.from_np(v.dtype), kind="ExternalInput").ap() for n, v in arrays.items()]
    out = nc.dram_tensor("out", [TOKENS, H], F32, kind="ExternalOutput").ap()
    xattn_moe(nc, *args, out)
    r = run(nc, [arrays], core_ids=[0])
    return r.results[0]["out"].reshape(B, S, H)
```
